# Optimizing a Trainium2 kernel written in Bass

```python
import numpy as np
import jax
import jax.numpy as jnp

def _softmax(x, axis=-1):
    return jax.nn.softmax(x, axis=axis)

def _gelu(x):
    return jax.nn.gelu(x, approximate=True)

def _silu(x):
    return jax.nn.silu(x)

def _sigmoid(x):
    return jax.nn.sigmoid(x)

def _layernorm(x, axis=-1, eps=1e-05):
    m = jnp.mean(x, axis=axis, keepdims=True)
    v = jnp.var(x, axis=axis, keepdims=True)
    return (x - m) / jnp.sqrt(v + eps)

def _scatter_add(tgt, idx, src, axis=0):
    return tgt.at[idx].add(src)

def _segment_sum(src, seg, n):
    return jax.ops.segment_sum(src, seg, n)
kernel_name = 'mk_flamingo_gated_d1_seqx_r8_4f330a'

def setup_inputs(seed: int=0):
    np.random.seed(seed)
    _w = jnp.asarray

    def _rec_inputs():
        import jax
        import jax.numpy as jnp
        _rk = jax.random.key(seed)
        x = -0.0003929 + 0.9999 * jax.random.normal(jax.random.fold_in(_rk, 1), (4, 256, 256), jnp.float32)
        _lenS = 256 - jax.random.randint(jax.random.fold_in(_rk, 7), (4,), 0, max(1, 256 // 4) + 1, jnp.int32)
        _lenS2 = 64 - jax.random.randint(jax.random.fold_in(_rk, 8), (4,), 0, max(1, 64 // 4) + 1, jnp.int32)
        _ctx_1024P = jax.random.normal(jax.random.fold_in(_rk, 11), (4, 16, 128), jnp.float32)
        _ctx_1024c = jax.random.dirichlet(jax.random.fold_in(_rk, 511), 0.3 * jnp.ones((16,), jnp.float32), (4, 64))
        _ctx_1024t = jnp.einsum('bsk,bkd->bsd', _ctx_1024c, _ctx_1024P)
        _ctx_1024t = _ctx_1024t * jax.lax.rsqrt(jnp.mean(jnp.square(_ctx_1024t)) + 1e-12) * 0.953939
        ctx_1024 = -0.000494167 + 1.00018 * (_ctx_1024t + 0.3 * jax.random.normal(jax.random.fold_in(_rk, 611), (4, 64, 128), jnp.float32))
        _validS = jnp.arange(256)[None, :] < _lenS[:, None]
        _validS2 = jnp.arange(64)[None, :] < _lenS2[:, None]
        _causal = jnp.tril(jnp.ones((256, 256), dtype=bool))
        mask_BxS2_bf1 = jnp.ones((4, 64), dtype=bool)
        _g = jax.random.normal(jax.random.fold_in(_rk, 9001), (2, 1), jnp.float32)
        _g = jnp.sign(_g) * jnp.maximum(jnp.abs(_g), 1.0) + (_g == 0) * 1.0
        g_xattn = _g[0]
        g_ffn = _g[1]
        return (x, ctx_1024, mask_BxS2_bf1, g_xattn, g_ffn)
    x, ctx_1024, mask_BxS2_bf1, g_xattn, g_ffn = _rec_inputs()

    def _L0_xattn_setup():
        import jax, jax.numpy as jnp
        import numpy as np
        N_HEADS = 16
        N_KV_HEADS = 8
        HEAD_DIM = 128
        D_TEXT = 256
        D_VISION = 128
        GROUPS = N_HEADS // N_KV_HEADS
        key = jax.random.key(seed)
        ks = jax.random.split(key, 6)
        B, T_text, T_vis = (4, 256, 72)
        text_hidden = jax.random.normal(ks[0], (B, T_text, D_TEXT), dtype=jnp.float32)
        vision_tokens = jax.random.normal(ks[1], (B, T_vis, D_VISION), dtype=jnp.float32)
        vision_mask = jnp.ones((B, T_vis), dtype=bool)
        s = 0.02
        Wq = jax.random.normal(ks[2], (D_TEXT, N_HEADS * HEAD_DIM), dtype=jnp.float32) * s
        Wk = jax.random.normal(ks[3], (D_VISION, N_KV_HEADS * HEAD_DIM), dtype=jnp.float32) * s
        Wv = jax.random.normal(ks[4], (D_VISION, N_KV_HEADS * HEAD_DIM), dtype=jnp.float32) * s
        Wo = jax.random.normal(ks[5], (N_HEADS * HEAD_DIM, D_TEXT), dtype=jnp.float32) * s
        return {'text_hidden': text_hidden, 'vision_tokens': vision_tokens, 'vision_mask': vision_mask, 'Wq': Wq, 'Wk': Wk, 'Wv': Wv, 'Wo': Wo}
    _L0_xattn_all = _L0_xattn_setup()
    _L0_xattn_in = {k: v for k, v in _L0_xattn_all.items() if k in ('Wq', 'Wk', 'Wv', 'Wo')}
    del _L0_xattn_all

    def _L0_ffn_setup():
        import jax, jax.numpy as jnp
        import numpy as np
        B, S, D = (2, 512, 256)
        H = 512
        HS = H // 2
        E = 4
        TOPK = 2
        SCALE = 0.02

        def _swiglu(xt, wu, wg, wd):
            return jax.nn.silu(xt @ wu.T) * (xt @ wg.T) @ wd.T
        key = jax.random.key(seed)
        ks = jax.random.split(key, 8)
        return {'x': jax.random.normal(ks[0], (B, S, D), dtype=jnp.float32), 'gate_w': jax.random.normal(ks[1], (E, D), dtype=jnp.float32) * SCALE, 'w1': jax.random.normal(ks[2], (E, H, D), dtype=jnp.float32) * SCALE, 'w3': jax.random.normal(ks[3], (E, H, D), dtype=jnp.float32) * SCALE, 'w2': jax.random.normal(ks[4], (E, D, H), dtype=jnp.float32) * SCALE, 'sw1': jax.random.normal(ks[5], (HS, D), dtype=jnp.float32) * SCALE, 'sw3': jax.random.normal(ks[6], (HS, D), dtype=jnp.float32) * SCALE, 'sw2': jax.random.normal(ks[7], (D, HS), dtype=jnp.float32) * SCALE}
    _L0_ffn_all = _L0_ffn_setup()
    _L0_ffn_in = {k: v for k, v in _L0_ffn_all.items() if k in ('gate_w', 'w1', 'w3', 'w2', 'sw1', 'sw3', 'sw2')}
    del _L0_ffn_all
    return {'x': x, 'ctx_1024': ctx_1024, 'mask_BxS2_bf1': mask_BxS2_bf1, 'g_xattn': g_xattn, 'g_ffn': g_ffn, 'L0_xattn_Wq': _L0_xattn_in['Wq'], 'L0_xattn_Wk': _L0_xattn_in['Wk'], 'L0_xattn_Wv': _L0_xattn_in['Wv'], 'L0_xattn_Wo': _L0_xattn_in['Wo'], 'L0_ffn_gate_w': _L0_ffn_in['gate_w'], 'L0_ffn_w1': _L0_ffn_in['w1'], 'L0_ffn_w3': _L0_ffn_in['w3'], 'L0_ffn_w2': _L0_ffn_in['w2'], 'L0_ffn_sw1': _L0_ffn_in['sw1'], 'L0_ffn_sw3': _L0_ffn_in['sw3'], 'L0_ffn_sw2': _L0_ffn_in['sw2']}

def reference(x, ctx_1024, mask_BxS2_bf1, g_xattn, g_ffn, L0_xattn_Wq, L0_xattn_Wk, L0_xattn_Wv, L0_xattn_Wo, L0_ffn_gate_w, L0_ffn_w1, L0_ffn_w3, L0_ffn_w2, L0_ffn_sw1, L0_ffn_sw3, L0_ffn_sw2):
    import jax
    import jax.numpy as jnp

    def _L0_xattn_ref(text_hidden, vision_tokens, vision_mask, Wq, Wk, Wv, Wo):
        import jax, jax.numpy as jnp
        import numpy as np
        N_HEADS = 16
        N_KV_HEADS = 8
        HEAD_DIM = 128
        D_TEXT = 256
        D_VISION = 128
        GROUPS = N_HEADS // N_KV_HEADS
        B, T_text, _ = text_hidden.shape
        T_vis = vision_tokens.shape[1]
        scale = jnp.float32(np.sqrt(HEAD_DIM))
        q = (text_hidden @ Wq).reshape(B, T_text, N_HEADS, HEAD_DIM).transpose(0, 2, 1, 3)
        k = (vision_tokens @ Wk).reshape(B, T_vis, N_KV_HEADS, HEAD_DIM).transpose(0, 2, 1, 3)
        v = (vision_tokens @ Wv).reshape(B, T_vis, N_KV_HEADS, HEAD_DIM).transpose(0, 2, 1, 3)
        k = jnp.repeat(k, GROUPS, axis=1)
        v = jnp.repeat(v, GROUPS, axis=1)
        scores = jnp.einsum('bhtd,bhsd->bhts', q, k) / scale
        mask = vision_mask[:, None, None, :]
        scores = jnp.where(mask, scores, -jnp.inf)
        attn = jax.nn.softmax(scores, axis=-1)
        attn = jnp.nan_to_num(attn, nan=0.0)
        out = jnp.einsum('bhts,bhsd->bhtd', attn, v)
        out = out.transpose(0, 2, 1, 3).reshape(B, T_text, N_HEADS * HEAD_DIM)
        return out @ Wo

    def _L0_ffn_ref(x, gate_w, w1, w3, w2, sw1, sw3, sw2):
        import jax, jax.numpy as jnp
        import numpy as np
        B, S, D = (2, 512, 256)
        H = 512
        HS = H // 2
        E = 4
        TOPK = 2
        SCALE = 0.02

        def _swiglu(xt, wu, wg, wd):
            return jax.nn.silu(xt @ wu.T) * (xt @ wg.T) @ wd.T
        orig_shape = x.shape
        xt = x.reshape(-1, orig_shape[-1])
        T = xt.shape[0]
        logits = xt @ gate_w.T
        probs = jax.nn.softmax(logits, axis=-1)
        topk_weight, topk_idx = jax.lax.top_k(probs, TOPK)
        rows = jnp.arange(T)[:, None]
        combine = jnp.zeros((T, E), dtype=x.dtype).at[rows, topk_idx].add(topk_weight)
        y = jnp.zeros_like(xt)
        for e in range(E):
            y = y + combine[:, e:e + 1] * _swiglu(xt, w1[e], w3[e], w2[e])
        y = y + _swiglu(xt, sw1, sw3, sw2)
        return y.reshape(orig_shape)
    x = x + jnp.tanh(g_xattn[0]) * _L0_xattn_ref(_layernorm(x, axis=-1), ctx_1024, mask_BxS2_bf1, L0_xattn_Wq, L0_xattn_Wk, L0_xattn_Wv, L0_xattn_Wo)
    x = x + jnp.tanh(g_ffn[0]) * _L0_ffn_ref(_layernorm(x, axis=-1), L0_ffn_gate_w, L0_ffn_w1, L0_ffn_w3, L0_ffn_w2, L0_ffn_sw1, L0_ffn_sw3, L0_ffn_sw2)
    return x

_drawn_inputs = setup_inputs


def setup_inputs(seed=0):
    import zlib

    import numpy as np

    out = dict(_drawn_inputs(seed))
    spreads = {}
    factors = {'L0_xattn_Wq': 8.0,
     'L0_xattn_Wk': 8.0,
     'L0_ffn_gate_w': 7.694,
     'L0_ffn_w1': 5.74,
     'L0_ffn_w3': 5.688,
     'L0_ffn_w2': 5.675,
     'L0_ffn_sw1': 3.607,
     'L0_ffn_sw3': 3.569,
     'L0_ffn_sw2': 3.569}
    for name, (base, spread) in spreads.items():
        noise = np.random.default_rng([zlib.crc32(name.encode()), seed]).standard_normal(out[name].shape)
        drawn = base * np.exp(spread * noise) if base else spread * noise
        out[name] = jnp.asarray(drawn.astype(out[name].dtype))
    for name, factor in factors.items():
        out[name] = (out[name] * factor).astype(out[name].dtype)
    return out
```

```python
from contextlib import ExitStack

import concourse.bass as bass
from concourse import mybir

F32 = mybir.dt.float32
F32R = mybir.dt.float32r
U8 = mybir.dt.uint8
ALU = mybir.AluOpType
ACT = mybir.ActivationFunctionType
AX = mybir.AxisListType

P = 128
NB, T, D = 4, 256, 256
S, DV = 64, 128
NH, NG, HD = 16, 8, 128
KD = D // P
NT = NB * T // P
TPB = T // P
NE, H, HS = 4, 512, 256
JE, JS = H // P, HS // P
NM = JS + NE * JE
WS = 4
RS = 2
HR = 4
CH = 512
TC = CH // P
NC = NB * T // CH
SW = NH * S
KVQ = 2 * HD + 2 * D
WOC = 2 * D
UPC = 2 * KD * P
FFC = UPC + D
SCALE = float(HD) ** -0.5
EPS = 1e-5
MASKED = 1e30


def wait(eng, sem, n):
    if isinstance(n, int) and n <= 0:
        return
    eng.wait_ge(sem, n)


def build(nc, x, ctxT, mask, gates, kvq, wo, gwT, ffn, ident_c, before_c, out):
    with ExitStack() as ctx:
        def sb(name, shape, dt=F32):
            return ctx.enter_context(nc.sbuf_tensor(name, shape, dt))

        def sem(name):
            return ctx.enter_context(nc.semaphore(name))

        x_sb = sb("x_sb", [P, NT * D])
        A_hi = sb("A_hi", [P, KD, NB, SW], F32R)
        A_lo = sb("A_lo", [P, KD, NB, SW], F32R)
        VO_hi = sb("VO_hi", [P, NB, NG, D], F32R)
        VO_lo = sb("VO_lo", [P, NB, NG, D], F32R)
        xT_hi = sb("xT_hi", [P, KD, NT * P], F32R)
        xT_lo = sb("xT_lo", [P, KD, NT * P], F32R)
        PT_hi = sb("PT_hi", [P, NG, P], F32R)
        PT_lo = sb("PT_lo", [P, NG, P], F32R)
        w_hi = sb("w_hi", [P, WS, FFC], F32R)
        w_lo = sb("w_lo", [P, WS, FFC], F32R)
        raw = sb("raw", [P, RS, FFC])
        probs = sb("probs", [P, TPB, SW])
        xn0 = sb("xn0", [P, TPB, D])
        ident = sb("ident", [P, P])
        before = sb("before", [P, NE * NE])
        mask_u8 = sb("mask_u8", [P, NB * S], U8)
        bias = sb("bias", [P, NB * S], F32R)
        onerow = sb("onerow", [P, P], F32R)
        anyvalid = sb("anyvalid", [P, NB])
        gates_sb = sb("gates_sb", [P, 2])
        tg = sb("tg", [P, 2])
        gw_sb = sb("gw_sb", [P, KD * NE])
        gw_hi = sb("gw_hi", [P, KD * NE], F32R)
        gw_lo = sb("gw_lo", [P, KD * NE], F32R)
        stats = sb("stats", [P, NT * 6])
        mv = sb("mv", [P, NT * 2])
        stats2 = sb("stats2", [P, NT * 6])
        mv2 = sb("mv2", [P, NT * 2])
        vare = sb("vare", [P, NT])
        vare2 = sb("vare2", [P, NT])
        rstd = sb("rstd", [P, NT])
        rstd2 = sb("rstd2", [P, NT])
        mhalf = sb("mhalf", [P, NT])
        mx = sb("mx", [P, TPB, NH])
        den = sb("den", [P, TPB, NH])
        rcp = sb("rcp", [P, TPB, NH])
        rden = sb("rden", [P, TPB, NH])
        logits = sb("logits", [P, NT, NE])
        lmax = sb("lmax", [P, NT])
        lexp = sb("lexp", [P, NT, NE])
        lsum = sb("lsum", [P, NT])
        lrcp = sb("lrcp", [P, NT])
        rp = sb("rp", [P, NT, NE])
        gt = sb("gt", [P, NT, NE * NE])
        eq = sb("eq", [P, NT, NE * NE])
        rank = sb("rank", [P, NT, NE])
        keep = sb("keep", [P, NT, NE])
        comb = sb("comb", [P, (1 + NE) * NT])

        raw_kvq = raw
        raw_wo = probs[:, 0, :].rearrange("p (s n) -> p s n", s=2)
        VT = probs[:, 1, 0:2 * NB * S].rearrange("p (s n) -> p s n", s=2)
        ctx_sb = probs[:, 1, 2 * NB * S:3 * NB * S]
        KT_hi = PT_hi[:, 0:4, :].rearrange("p (s a) n -> p s (a n)", s=2)
        KT_lo = PT_lo[:, 0:4, :].rearrange("p (s a) n -> p s (a n)", s=2)
        mask_f = xn0[:, 0, :]
        xn1 = probs[:, 0, 0:TPB * D].rearrange("p (t d) -> p t d", d=D)
        xn = [xn0, xn1]
        hid_hi = A_hi[:, 0, 0:HR * CH // SW, :].rearrange("p a (b n) -> p (a b) n", n=CH)
        hid_lo = A_lo[:, 0, 0:HR * CH // SW, :].rearrange("p a (b n) -> p (a b) n", n=CH)
        silu_sb = probs[:, 0, :].rearrange("p (s n) -> p s n", s=2)
        hid_f = probs[:, 1, :].rearrange("p (s n) -> p s n", s=2)

        bankP, bankQ, bankR, bankS = [ctx.enter_context(nc.psum_tensor(f"bank{c}", [P, 2, 512], F32)) for c in "PQRS"]
        scores_ps = [bankP, bankQ]
        up_ps = [bankP, bankQ]
        acc_ps = [bankR, bankS]

        ctx_ld, x_ld, const_ld = sem("ctx_ld"), sem("x_ld"), sem("const_ld")
        kvq_ld = [sem(f"kvq_ld{i}") for i in range(2)]
        wo_ld = [sem(f"wo_ld{i}") for i in range(2)]
        ffn_ld = [sem(f"ffn_ld{i}") for i in range(RS)]
        prep = sem("prep")
        onerow_ok, tg_ok = sem("onerow_ok"), sem("tg_ok")
        gwhi_ok, gwlo_ok = sem("gwhi_ok"), sem("gwlo_ok")
        kv_ps, k_hi, kv_sb = sem("kv_ps"), sem("k_hi"), sem("kv_sb")
        wq_hi, wq_lo = sem("wq_hi"), sem("wq_lo")
        a_ps, a_hi, a_lo = sem("a_ps"), sem("a_hi"), sem("a_lo")
        vo_ps, vo_hi, vo_lo = sem("vo_ps"), sem("vo_hi"), sem("vo_lo")
        st1, vare_ok, rstd_ok, mhalf_ok = sem("st1"), sem("vare_ok"), sem("rstd_ok"), sem("mhalf_ok")
        xn_ok, xt_ps, xt_hi, xt_lo = sem("xn_ok"), sem("xt_ps"), sem("xt_hi"), sem("xt_lo")
        sc_ps, mx_ok, sub_ok, exp_ok = sem("sc_ps"), sem("mx_ok"), sem("sub_ok"), sem("exp_ok")
        den_ok, rcp_ok, rden_ok, p_ok = sem("den_ok"), sem("rcp_ok"), sem("rden_ok"), sem("p_ok")
        pt_ps, pt_hi, pt_lo = sem("pt_ps"), sem("pt_hi"), sem("pt_lo")
        pv_ps, x1_ok, st2, mv2_ok = sem("pv_ps"), sem("x1_ok"), sem("st2"), sem("mv2_ok")
        vare2_ok, rstd2_ok = sem("vare2_ok"), sem("rstd2_ok")
        xn2_ok, x2_ps, x2_hi, x2_lo = sem("xn2_ok"), sem("x2_ps"), sem("x2_hi"), sem("x2_lo")
        lg_ps, route, lexp_ok = sem("lg_ps"), sem("route"), sem("lexp_ok")
        wf_hi, wf_lo = sem("wf_hi"), sem("wf_lo")
        u_ps, g_ps, silu_ok, hid_ok = sem("u_ps"), sem("g_ps"), sem("silu_ok"), sem("hid_ok")
        hid_hi_ok, hid_lo_ok = sem("hid_hi_ok"), sem("hid_lo_ok")
        down_ps, y_ok, stored = sem("down_ps"), sem("y_ok"), sem("stored")

        def split3(eng, acc, l_hi, l_lo, r_hi, r_lo, start, stop, **kw):
            eng.matmul(acc, l_hi, r_hi, start=start, stop=False, **kw)
            eng.matmul(acc, l_hi, r_lo, start=False, stop=False, **kw)
            return eng.matmul(acc, l_lo, r_hi, start=False, stop=stop, **kw)

        def by_head(ap):
            return ap.rearrange("p (h s) -> p h s", s=S)

        def xtile(n):
            return x_sb[:, bass.ds(n * D, D)]

        block = ctx.enter_context(nc.Block())

        @block.sync
        def _(sp):
            def load_head(g, s, n):
                wait(sp, kv_ps, g - 1)
                wait(sp, wq_lo, g - 1)
                sp.dma_start(raw_kvq[:, s, :], kvq[bass.ds(g, 1), :, :].rearrange("g p n -> p (g n)")).then_inc(kvq_ld[s], 16)
                wait(sp, vo_ps, (g - 1) * 2)
                sp.dma_start(raw_wo[:, s, :], wo[bass.ds(g, 1), :, :].rearrange("g p n -> p (g n)")).then_inc(wo_ld[s], 16)

            def load_ffn(m, s):
                wait(sp, wf_lo, m - RS + 1)
                sp.dma_start(raw[:, s, :], ffn[bass.ds(m, 1), :, :].rearrange("g p n -> p (g n)")).then_inc(ffn_ld[s], 16)

            sp.dma_start(ctx_sb[:, :], ctxT).then_inc(ctx_ld, 16)
            load_head(0, 0, 0)
            load_head(1, 1, 0)
            sp.dma_start(gates_sb[:, :], gates).then_inc(const_ld, 16)
            sp.dma_start(mask_u8[:, :], mask).then_inc(const_ld, 16)
            sp.dma_start(ident[:, :], ident_c).then_inc(const_ld, 16)
            sp.dma_start(before[:, :], before_c).then_inc(const_ld, 16)
            sp.dma_start(gw_sb[:, :], gwT).then_inc(const_ld, 16)
            sp.dma_start(x_sb[:, :].rearrange("p (t d) -> p t d", d=D), x.rearrange("(t p) d -> p t d", p=P)).then_inc(x_ld, 16)
            with sp.Fori(1, NG // 2) as it:
                for s in range(2):
                    load_head(it * 2 + s, s, it)
            sp.wait_ge(wq_lo, NG)
            sp.wait_ge(vo_ps, 2 * NG)
            for s in range(RS):
                load_ffn(s, s)
            with sp.Fori(1, NM // RS) as it:
                for s in range(RS):
                    load_ffn(it * RS + s, s)
            for c in range(NC):
                sp.wait_ge(y_ok, NE * NC + c + 1)
                sp.dma_start(out.rearrange("(t p) d -> p t d", p=P)[:, c * TC:(c + 1) * TC, :],
                             x_sb[:, c * TC * D:(c + 1) * TC * D].rearrange("p (t d) -> p t d", d=D)).then_inc(stored, 16)
            sp.wait_ge(stored, 16 * NC)

        @block.tensor
        def _(pe):
            def keys_values(g, s, n):
                pe.wait_ge(kvq_ld[s], (n + 1) * 16)
                wait(pe, kv_sb, g - 1)
                pe.matmul(bankP[:, s, 0:NB * S], raw_kvq[:, s, 0:HD], ctx_sb[:, :], start=True, stop=True)
                pe.matmul(bankP[:, s, NB * S:], raw_kvq[:, s, HD:2 * HD], ctx_sb[:, :], start=True, stop=True).then_inc(kv_ps, 1)

            def query_side(g, s):
                pe.wait_ge(kv_sb, g + 1)
                pe.wait_ge(wq_lo, g + 1)
                for hh in range(2):
                    wait(pe, a_lo, (g - 1) * 2 + hh + 1)
                    for k in range(KD):
                        c = hh * D + k * P
                        mm = split3(pe, bankQ[:, hh, k * D:(k + 1) * D], w_hi[:, s, c:c + P], w_lo[:, s, c:c + P],
                                    KT_hi[:, s, :], KT_lo[:, s, :], True, True)
                    mm.then_inc(a_ps, 1)

            def output_side(g, s, n):
                pe.wait_ge(wo_ld[s], (n + 1) * 16)
                for pair in range(2):
                    wait(pe, vo_lo, (g - 1) * 2 + pair + 1)
                    for r in range(2):
                        b = pair * 2 + r
                        for hh in range(2):
                            mm = pe.matmul(bankR[hh * S:(hh + 1) * S, pair, r * D:(r + 1) * D], VT[:, s, b * S:(b + 1) * S],
                                           raw_wo[:, s, hh * D:(hh + 1) * D], start=True, stop=True)
                    mm.then_inc(vo_ps, 1)

            def heads(it, last):
                g = it * 2
                keys_values(g + 1, 1, it)
                query_side(g, 0)
                output_side(g, 0, it)
                if not last:
                    keys_values(g + 2, 0, it + 1)
                query_side(g + 1, 1)
                output_side(g + 1, 1, it)

            def turn_x(b):
                pe.wait_ge(xn_ok, b + 1)
                wait(pe, xt_lo, b)
                for par in range(TPB):
                    for k in range(KD):
                        c = (par * KD + k) * P
                        mm = pe.transpose(bankS[:, 0, c:c + P], xn0[:, par, k * P:(k + 1) * P], ident[:, :])
                mm.then_inc(xt_ps, 1)

            def scores(b, par):
                n = b * TPB + par
                pe.wait_ge(xt_lo, b + 1)
                wait(pe, sub_ok, n - 1)
                for hf in range(2):
                    acc = scores_ps[par][:, hf, :]
                    pe.matmul(acc, onerow[:, :], bias[:, bass.ds(b * S, S)].unsqueeze(1).to_broadcast([P, NH // 2, S]),
                              start=True, stop=False)
                    for k in range(KD):
                        mm = split3(pe, acc, xT_hi[:, k, par * P:(par + 1) * P], xT_lo[:, k, par * P:(par + 1) * P],
                                    A_hi[:, k, bass.ds(b, 1), hf * 512:(hf + 1) * 512].rearrange("p a n -> p (a n)"),
                                    A_lo[:, k, bass.ds(b, 1), hf * 512:(hf + 1) * 512].rearrange("p a n -> p (a n)"),
                                    False, k == KD - 1)
                mm.then_inc(sc_ps, 1)

            def turn_p(b, par):
                n = b * TPB + par
                pe.wait_ge(p_ok, n + 1)
                for q in range(2):
                    for g in range(NG // 2):
                        c = (q * NG // 2 + g) * P
                        mm = pe.transpose(bankR[:, q, g * P:(g + 1) * P], probs[:, par, c:c + P], ident[:, :])
                    mm.then_inc(pt_ps, 1)

            def attend(b, par):
                n = b * TPB + par
                for g in range(NG):
                    if g % (NG // 2) == 0:
                        pe.wait_ge(pt_lo, n * 2 + g // (NG // 2) + 1)
                    mm = split3(pe, bankS[:, 1, 0:D], PT_hi[:, g, :], PT_lo[:, g, :],
                                VO_hi[:, bass.ds(b, 1), g, :].rearrange("p a n -> p (a n)"),
                                VO_lo[:, bass.ds(b, 1), g, :].rearrange("p a n -> p (a n)"), g == 0, g == NG - 1)
                mm.then_inc(pv_ps, 1)

            def attend_batch(b, last):
                turn_p(b - 1, 0)
                scores(b, 0)
                attend(b - 1, 0)
                turn_p(b - 1, 1)
                scores(b, 1)
                if not last:
                    turn_x(b + 1)
                attend(b - 1, 1)

            def turn_x2(c, bank):
                pe.wait_ge(xn2_ok, c + 1)
                for par in range(TPB):
                    for k in range(KD):
                        o = (par * KD + k) * P
                        mm = pe.transpose(bank[:, c % 2, o:o + P], xn[c % 2][:, par, k * P:(k + 1) * P], ident[:, :])
                mm.then_inc(x2_ps, 1)

            def up_unit(n, u, s):
                c = u % 2
                for mat, done in ((0, u_ps), (1, g_ps)):
                    for k in range(KD):
                        o = (mat * KD + k) * P
                        mm = split3(pe, up_ps[c][:, mat, :], w_hi[:, s, o:o + P], w_lo[:, s, o:o + P],
                                    xT_hi[:, k, c * CH:(c + 1) * CH], xT_lo[:, k, c * CH:(c + 1) * CH], k == 0, k == KD - 1)
                    mm.then_inc(done, 1)

            def down_unit(n, u, s, first, last, e):
                c = u % 2
                pe.wait_ge(hid_lo_ok, n + 1)
                if first:
                    wait(pe, y_ok, (e - 1) * NC + c + 1)
                for tt in range(TC):
                    o = tt * P
                    mm = split3(pe, acc_ps[c][:, tt // 2, tt % 2 * D:(tt % 2 + 1) * D],
                                hid_hi[:, u % HR, o:o + P], hid_lo[:, u % HR, o:o + P],
                                w_hi[:, s, UPC:FFC], w_lo[:, s, UPC:FFC],
                                first and tt % 2 == 0, last, skip_group_check=True)
                mm.then_inc(down_ps, 1)

            pe.wait_ge(ctx_ld, 16)
            keys_values(0, 0, 0)
            heads(0, False)
            with pe.Fori(1, NG // 2 - 1) as it:
                heads(it, False)
            pe.wait_ge(const_ld, 80)
            turn_x(0)
            heads(NG // 2 - 1, True)
            pe.wait_ge(onerow_ok, 1)
            pe.wait_ge(kv_sb, NG)
            pe.wait_ge(a_lo, 2 * NG)
            scores(0, 0)
            scores(0, 1)
            turn_x(1)
            pe.wait_ge(vo_lo, 2 * NG)
            with pe.Fori(1, NB - 1) as b:
                attend_batch(b, False)
            attend_batch(NB - 1, True)
            turn_p(NB - 1, 0)
            pe.wait_ge(sub_ok, NT)
            turn_x2(0, bankP)
            turn_x2(1, bankP)
            attend(NB - 1, 0)
            turn_p(NB - 1, 1)
            attend(NB - 1, 1)
            pe.wait_ge(wf_lo, 1)
            pe.wait_ge(x2_lo, 2)
            up_unit(0, 0, JS)
            pe.wait_ge(x1_ok, NT)
            turn_x2(2, bankS)
            turn_x2(3, bankS)
            pe.wait_ge(gwlo_ok, 1)
            pe.wait_ge(pt_lo, 2 * NT)
            for t in range(NT):
                if t == NT // 2:
                    pe.wait_ge(x2_lo, 4)
                for k in range(KD):
                    l_hi, l_lo = (w[:, k, t * P:(t + 1) * P] for w in (xT_hi, xT_lo))
                    r_hi, r_lo = (w[:, k * NE:(k + 1) * NE] for w in (gw_hi, gw_lo))
                    split3(pe, bankR[:, 0, t * NE:(t + 1) * NE], l_hi, l_lo, r_hi, r_lo, k == 0, False)
                    mm = pe.matmul(bankR[:, 0, t * NE:(t + 1) * NE], l_lo, r_lo, start=False, stop=k == KD - 1)
            mm.then_inc(lg_ps, 1)
            up_unit(1, 1, JS)
            pe.wait_ge(wf_lo, 2)
            for n in (2, 3):
                pe.wait_ge(hid_ok, n - 1)
                up_unit(n, n, JS + 1)
                if n == 2:
                    pe.wait_ge(route, 1)
                down_unit(n - 2, n - 2, JS, True, False, 0)

            def expert(e):
                base = e * 8 + 2 * JS
                for u in range(2 * JE):
                    n = base + u
                    pe.wait_ge(wf_lo, e * JE + JS + u // 2 + 1)
                    pe.wait_ge(hid_ok, n - 1)
                    up_unit(n, u, u // 2)
                    if u < 2:
                        down_unit(n - 2, u + 2 * JE - 2, WS - 1, False, True, e)
                    else:
                        down_unit(n - 2, u - 2, u // 2 - 1, u < 4, False, e + 1)

            with pe.Fori(0, NE) as e:
                expert(e)
            for u in range(2):
                n = 2 * NM - 2 + u
                down_unit(n, u + 2 * JE - 2, WS - 1, False, True, NE)

        @block.scalar
        def _(act):
            def split_wq(g, s, n):
                act.wait_ge(kvq_ld[s], (n + 1) * 16)
                wait(act, a_ps, (g - 1) * 2)
                act.copy(w_hi[:, s, 0:2 * D], raw_kvq[:, s, 2 * HD:KVQ]).then_inc(wq_hi, 1)

            def split_k(g, s):
                act.wait_ge(kv_ps, g + 1)
                act.copy(KT_hi[:, s, :], bankP[:, s, 0:NB * S]).then_inc(k_hi, 1)

            def evict_head(g):
                for hh in range(2):
                    act.wait_ge(a_ps, g * 2 + hh + 1)
                    act.copy(A_hi[:, :, :, bass.ds(g * 2 * S + hh * S, S)],
                             bankQ[:, hh, :].rearrange("p (k b s) -> p k b s", k=KD, b=NB)).then_inc(a_hi, 1)
                for pair in range(2):
                    act.wait_ge(vo_ps, g * 2 + pair + 1)
                    act.copy(VO_hi[:, pair * 2:pair * 2 + 2, bass.ds(g, 1), :].rearrange("p b a n -> p b (a n)"),
                             bankR[:, pair, :].rearrange("p (b n) -> p b n", b=2)).then_inc(vo_hi, 1)

            def heads(it, last):
                g = it * 2
                split_wq(g + 1, 1, it)
                split_k(g + 1, 1)
                evict_head(g)
                if not last:
                    split_wq(g + 2, 0, it + 1)
                    split_k(g + 2, 0)
                evict_head(g + 1)

            def split_x(b):
                act.wait_ge(xt_ps, b + 1)
                wait(act, sc_ps, b * TPB)
                act.copy(xT_hi[:, :, 0:TPB * P].rearrange("p k (t n) -> p t k n", n=P),
                         bankS[:, 0, :].rearrange("p (t k n) -> p t k n", t=TPB, k=KD)).then_inc(xt_hi, 1)

            def exponent(b, par):
                act.wait_ge(sub_ok, b * TPB + par + 1)
                act.activation(probs[:, par, :], probs[:, par, :], ACT.Exp, scale=SCALE).then_inc(exp_ok, 1)

            def split_p(b, par):
                n = b * TPB + par
                for q in range(2):
                    act.wait_ge(pt_ps, n * 2 + q + 1)
                    act.copy(PT_hi[:, q * NG // 2:(q + 1) * NG // 2, :],
                             bankR[:, q, :].rearrange("p (g n) -> p g n", n=P)).then_inc(pt_hi, 1)

            def attend_batch(b, last):
                split_p(b - 1, 0)
                exponent(b, 0)
                split_p(b - 1, 1)
                if not last:
                    split_x(b + 1)
                exponent(b, 1)

            def split_x2(c, bank):
                act.wait_ge(x2_ps, c + 1)
                act.copy(xT_hi[:, :, c * TPB * P:(c + 1) * TPB * P].rearrange("p k (t n) -> p t k n", n=P),
                         bank[:, c % 2, :].rearrange("p (t k n) -> p t k n", t=TPB, k=KD)).then_inc(x2_hi, 1)

            def split_w(m, s, r, n):
                act.wait_ge(ffn_ld[r], (n + 1) * 16)
                wait(act, down_ps, (m - WS) * 2 + 2)
                act.copy(w_hi[:, s, :], raw[:, r, :]).then_inc(wf_hi, 1)

            def silu(n, u):
                act.wait_ge(u_ps, n + 1)
                wait(act, hid_ok, n - 1)
                act.activation(silu_sb[:, u % 2, :], up_ps[u % 2][:, 0, :], ACT.Silu).then_inc(silu_ok, 1)

            def split_hid(n, u):
                act.wait_ge(hid_ok, n + 1)
                wait(act, down_ps, n - HR + 1)
                act.copy(hid_hi[:, u % HR, :], hid_f[:, u % 2, :]).then_inc(hid_hi_ok, 1)

            act.wait_ge(const_ld, 80)
            act.activation(tg[:, :], gates_sb[:, :], ACT.Tanh).then_inc(tg_ok, 1)
            act.copy(gw_hi[:, :], gw_sb[:, :]).then_inc(gwhi_ok, 1)
            split_wq(0, 0, 0)
            split_k(0, 0)
            heads(0, False)
            with act.Fori(1, NG // 2 - 1) as it:
                heads(it, False)
            split_x(0)
            heads(NG // 2 - 1, True)
            exponent(0, 0)
            exponent(0, 1)
            split_x(1)
            for m in range(JS):
                split_w(m, JS + m, m % RS, m // RS)
            with act.Fori(1, NB - 1) as b:
                attend_batch(b, False)
            attend_batch(NB - 1, True)
            split_p(NB - 1, 0)
            split_x2(0, bankP)
            split_x2(1, bankP)
            split_p(NB - 1, 1)
            split_x2(2, bankS)
            split_x2(3, bankS)
            act.wait_ge(route, 3)
            act.activation(lexp[:, :, :], logits[:, :, :], ACT.Exp).then_inc(lexp_ok, 1)
            for n in range(2 * JS):
                silu(n, n)
                if n >= 1:
                    split_hid(n - 1, n - 1)
                if n % 2 == 0:
                    m = JS + n // 2
                    split_w(m, n // 2, m % RS, m // RS)

            def expert(e, last):
                base = e * 8 + 2 * JS
                for u in range(2 * JE):
                    silu(base + u, u)
                    split_hid(base + u - 1, u - 1 + 2 * JE)
                    if u % 2 == 0 and not (last and u >= JE):
                        i = JS + u // 2 + 2
                        split_w(e * JE + i, (i + JS) % WS, i % RS, e * (JE // RS) + i // RS)

            with act.Fori(0, NE - 1) as e:
                expert(e, False)
            expert(NE - 1, True)
            split_hid(2 * NM - 1, 2 * JE - 1)

        @block.vector
        def _(dve):
            def split_kv(g, s):
                dve.wait_ge(k_hi, g + 1)
                dve.tensor_tensor(KT_lo[:, s, :], bankP[:, s, 0:NB * S], KT_hi[:, s, :].bitcast(F32), ALU.subtract)
                wait(dve, vo_ps, (g - 1) * 2)
                dve.tensor_copy(VT[:, s, :], bankP[:, s, NB * S:]).then_inc(kv_sb, 1)

            def evict_head(g):
                for hh in range(2):
                    dve.wait_ge(a_hi, g * 2 + hh + 1)
                    o = bass.ds(g * 2 * S + hh * S, S)
                    for k in range(KD):
                        ins = dve.tensor_tensor(A_lo[:, k, :, o], bankQ[:, hh, k * D:(k + 1) * D].rearrange("p (b s) -> p b s", b=NB),
                                                A_hi[:, k, :, o].bitcast(F32), ALU.subtract)
                    ins.then_inc(a_lo, 1)
                for pair in range(2):
                    dve.wait_ge(vo_hi, g * 2 + pair + 1)
                    dve.tensor_tensor(VO_lo[:, pair * 2:pair * 2 + 2, bass.ds(g, 1), :].rearrange("p b a n -> p b (a n)"),
                                      bankR[:, pair, :].rearrange("p (b n) -> p b n", b=2),
                                      VO_hi[:, pair * 2:pair * 2 + 2, bass.ds(g, 1), :].rearrange("p b a n -> p b (a n)").bitcast(F32),
                                      ALU.subtract).then_inc(vo_lo, 1)

            def heads(it, last):
                g = it * 2
                split_kv(g + 1, 1)
                evict_head(g)
                if not last:
                    split_kv(g + 2, 0)
                evict_head(g + 1)

            def normal_x(b):
                wait(dve, xt_ps, b)
                for par in range(TPB):
                    n = b * TPB + par
                    ins = dve.tensor_scalar(xn0[:, par, :], xtile(n), mv[:, bass.ds(n * 2, 1)], rstd[:, bass.ds(n, 1)],
                                            ALU.subtract, ALU.mult)
                ins.then_inc(xn_ok, 1)

            def split_x(b):
                dve.wait_ge(xt_hi, b + 1)
                for par in range(TPB):
                    o = slice(par * P, (par + 1) * P)
                    ins = dve.tensor_tensor(xT_lo[:, :, o], bankS[:, 0, par * D:(par + 1) * D].rearrange("p (k n) -> p k n", k=KD),
                                            xT_hi[:, :, o].bitcast(F32), ALU.subtract)
                ins.then_inc(xt_lo, 1)

            def less_max(b, par):
                n = b * TPB + par
                dve.wait_ge(sc_ps, n + 1)
                sc = scores_ps[par][:, :, :].rearrange("p a (h s) -> p (a h) s", s=S)
                dve.tensor_reduce(mx[:, par, :], sc, AX.X, ALU.max).then_inc(mx_ok, 1)
                dve.wait_ge(mx_ok, n + 1)
                wait(dve, pt_ps, (n - 1) * 2)
                dve.tensor_tensor(by_head(probs[:, par, :]), sc, mx[:, par, :].unsqueeze(2).to_broadcast([P, NH, S]),
                                  ALU.subtract).then_inc(sub_ok, 1)

            def denominator(b, par):
                n = b * TPB + par
                dve.wait_ge(exp_ok, n + 1)
                wait(dve, p_ok, n - 1)
                dve.tensor_reduce(den[:, par, :], by_head(probs[:, par, :]), AX.X, ALU.add).then_inc(den_ok, 1)
                dve.wait_ge(den_ok, n + 1)
                dve.reciprocal(rcp[:, par, :], den[:, par, :]).then_inc(rcp_ok, 1)
                dve.wait_ge(rcp_ok, n + 1)
                dve.tensor_scalar(rden[:, par, :], rcp[:, par, :], anyvalid[:, bass.ds(b, 1)], None, ALU.mult).then_inc(rden_ok, 1)

            def split_p(b, par):
                n = b * TPB + par
                for q in range(2):
                    dve.wait_ge(pt_hi, n * 2 + q + 1)
                    o = slice(q * NG // 2, (q + 1) * NG // 2)
                    dve.tensor_tensor(PT_lo[:, o, :], bankR[:, q, :].rearrange("p (g n) -> p g n", n=P),
                                      PT_hi[:, o, :].bitcast(F32), ALU.subtract).then_inc(pt_lo, 1)

            def add_attention(b, par):
                n = b * TPB + par
                dve.wait_ge(pv_ps, n + 1)
                dve.scalar_tensor_tensor(xtile(n), bankS[:, 1, 0:D], tg[:, 0:1], xtile(n), ALU.mult, ALU.add).then_inc(x1_ok, 1)
                dve.wait_ge(x1_ok, n + 1)
                dve.bn_stats(stats2[:, bass.ds(n * 6, 6)], xtile(n)).then_inc(st2, 1)

            def attend_batch(b, last):
                split_p(b - 1, 0)
                less_max(b, 0)
                add_attention(b - 1, 0)
                denominator(b, 0)
                if not last:
                    normal_x(b + 1)
                split_p(b - 1, 1)
                less_max(b, 1)
                if not last:
                    split_x(b + 1)
                add_attention(b - 1, 1)
                denominator(b, 1)

            def variance2(h):
                dve.wait_ge(st2, (h + 1) * NT // 2)
                for n in range(h * NT // 2, (h + 1) * NT // 2):
                    dve.bn_aggr(mv2[:, n * 2:n * 2 + 2], stats2[:, n * 6:n * 6 + 6]).then_inc(mv2_ok, 1)
                dve.wait_ge(mv2_ok, (h + 1) * NT // 2)
                o = slice(h * NT // 2, (h + 1) * NT // 2)
                dve.tensor_scalar(vare2[:, o], mv2[:, :].rearrange("p (t c) -> p t c", c=2)[:, o, 1], EPS, None,
                                  ALU.add).then_inc(vare2_ok, 1)

            def normal_x2(c):
                dve.wait_ge(rstd2_ok, c // 2 + 1)
                wait(dve, x2_ps, c - 1)
                for par in range(TPB):
                    n = c * TPB + par
                    ins = dve.tensor_scalar(xn[c % 2][:, par, :], xtile(n), mv2[:, n * 2:n * 2 + 1], rstd2[:, n:n + 1],
                                            ALU.subtract, ALU.mult)
                ins.then_inc(xn2_ok, 1)

            def split_x2(c, bank):
                dve.wait_ge(x2_hi, c + 1)
                for par in range(TPB):
                    o = slice((c * TPB + par) * P, (c * TPB + par + 1) * P)
                    ins = dve.tensor_tensor(xT_lo[:, :, o], bank[:, c % 2, par * D:(par + 1) * D].rearrange("p (k n) -> p k n", k=KD),
                                            xT_hi[:, :, o].bitcast(F32), ALU.subtract)
                ins.then_inc(x2_lo, 1)

            def split_w(m, s, r):
                dve.wait_ge(wf_hi, m + 1)
                dve.tensor_tensor(w_lo[:, s, :], raw[:, r, :], w_hi[:, s, :].bitcast(F32), ALU.subtract).then_inc(wf_lo, 1)

            def gate_hidden(n, u):
                dve.wait_ge(silu_ok, n + 1)
                dve.wait_ge(g_ps, n + 1)
                wait(dve, hid_lo_ok, n - 1)
                dve.tensor_tensor(hid_f[:, u % 2, :], up_ps[u % 2][:, 1, :], silu_sb[:, u % 2, :], ALU.mult).then_inc(hid_ok, 1)

            def split_hid(n, u):
                dve.wait_ge(hid_hi_ok, n + 1)
                dve.tensor_tensor(hid_lo[:, u % HR, :], hid_f[:, u % 2, :], hid_hi[:, u % HR, :].bitcast(F32),
                                  ALU.subtract).then_inc(hid_lo_ok, 1)

            def add_expert(e, c):
                dve.wait_ge(down_ps, e * 8 + 2 * JS - 1 + c)
                for tt in range(TC):
                    t = c * TC + tt
                    ins = dve.scalar_tensor_tensor(x_sb[:, t * D:(t + 1) * D], acc_ps[c][:, tt // 2, tt % 2 * D:(tt % 2 + 1) * D],
                                                   comb[:, bass.ds(e * NT + t, 1)], x_sb[:, t * D:(t + 1) * D], ALU.mult, ALU.add)
                ins.then_inc(y_ok, 1)

            dve.memset(onerow[:, :].bitcast(F32), 0.0).then_inc(prep, 1)
            dve.wait_ge(prep, 1)
            dve.memset(onerow[0:1, :].bitcast(F32), 1.0).then_inc(onerow_ok, 1)
            dve.memset(mhalf[:, :], -0.5).then_inc(mhalf_ok, 1)
            dve.wait_ge(const_ld, 80)
            dve.tensor_copy(mask_f[:, :], mask_u8[:, :]).then_inc(prep, 1)
            dve.wait_ge(prep, 2)
            dve.tensor_scalar(bias[:, :], mask_f[:, :], -1.0, MASKED, ALU.add, ALU.mult)
            dve.tensor_reduce(anyvalid[:, :], mask_f[:, :].rearrange("p (b s) -> p b s", s=S), AX.X, ALU.max)
            dve.wait_ge(gwhi_ok, 1)
            dve.tensor_tensor(gw_lo[:, :], gw_sb[:, :], gw_hi[:, :].bitcast(F32), ALU.subtract).then_inc(gwlo_ok, 1)
            split_kv(0, 0)
            heads(0, False)
            dve.wait_ge(x_ld, 16)
            for n in range(NT):
                dve.bn_stats(stats[:, n * 6:n * 6 + 6], xtile(n)).then_inc(st1, 1)
            for n in range(NT):
                dve.wait_ge(st1, n + 1)
                dve.bn_aggr(mv[:, n * 2:n * 2 + 2], stats[:, n * 6:n * 6 + 6]).then_inc(st1, 1)
            dve.wait_ge(st1, 2 * NT)
            dve.tensor_scalar(vare[:, :], mv[:, :].rearrange("p (t c) -> p t c", c=2)[:, :, 1], EPS, None, ALU.add).then_inc(vare_ok, 1)
            with dve.Fori(1, NG // 2 - 1) as it:
                heads(it, False)
            dve.wait_ge(rstd_ok, 1)
            normal_x(0)
            split_x(0)
            normal_x(1)
            heads(NG // 2 - 1, True)
            less_max(0, 0)
            denominator(0, 0)
            less_max(0, 1)
            split_x(1)
            denominator(0, 1)
            dve.wait_ge(tg_ok, 1)
            for m in range(JS):
                split_w(m, JS + m, m % RS)
            with dve.Fori(1, NB - 1) as b:
                attend_batch(b, False)
            variance2(0)
            attend_batch(NB - 1, True)
            split_p(NB - 1, 0)
            normal_x2(0)
            normal_x2(1)
            split_x2(0, bankP)
            split_x2(1, bankP)
            add_attention(NB - 1, 0)
            split_p(NB - 1, 1)
            add_attention(NB - 1, 1)
            variance2(1)
            normal_x2(2)
            normal_x2(3)
            split_x2(2, bankS)
            split_x2(3, bankS)
            dve.wait_ge(lg_ps, 1)
            dve.tensor_copy(logits[:, :, :], bankR[:, 0, 0:NT * NE].rearrange("p (t e) -> p t e", e=NE)).then_inc(route, 1)
            dve.wait_ge(route, 1)
            dve.tensor_reduce(lmax[:, :], logits[:, :, :], AX.X, ALU.max).then_inc(route, 1)
            dve.wait_ge(route, 2)
            dve.tensor_tensor(logits[:, :, :], logits[:, :, :], lmax[:, :].unsqueeze(2).to_broadcast([P, NT, NE]),
                              ALU.subtract).then_inc(route, 1)
            dve.wait_ge(lexp_ok, 1)
            dve.tensor_reduce(lsum[:, :], lexp[:, :, :], AX.X, ALU.add).then_inc(route, 1)
            dve.wait_ge(route, 4)
            dve.reciprocal(lrcp[:, :], lsum[:, :]).then_inc(route, 1)
            dve.wait_ge(route, 5)
            dve.tensor_tensor(rp[:, :, :], lexp[:, :, :], lrcp[:, :].unsqueeze(2).to_broadcast([P, NT, NE]),
                              ALU.mult).then_inc(route, 1)
            dve.wait_ge(route, 6)
            pj = rp[:, :, :].unsqueeze(2).to_broadcast([P, NT, NE, NE])
            pe_ = rp[:, :, :].unsqueeze(3).to_broadcast([P, NT, NE, NE])
            four = lambda a: a[:, :, :].rearrange("p t (e j) -> p t e j", e=NE)
            dve.tensor_tensor(four(gt), pj, pe_, ALU.is_gt).then_inc(route, 1)
            dve.tensor_tensor(four(eq), pj, pe_, ALU.is_equal).then_inc(route, 1)
            dve.wait_ge(route, 8)
            dve.tensor_tensor(eq[:, :, :], eq[:, :, :], before[:, :].unsqueeze(1).to_broadcast([P, NT, NE * NE]),
                              ALU.mult).then_inc(route, 1)
            dve.wait_ge(route, 9)
            dve.tensor_tensor(gt[:, :, :], gt[:, :, :], eq[:, :, :], ALU.add).then_inc(route, 1)
            dve.wait_ge(route, 10)
            dve.tensor_reduce(rank[:, :, :], four(gt), AX.X, ALU.add).then_inc(route, 1)
            dve.wait_ge(route, 11)
            dve.tensor_scalar(keep[:, :, :], rank[:, :, :], 2.0, tg[:, 1:2], ALU.is_lt, ALU.mult).then_inc(route, 1)
            dve.tensor_scalar(comb[:, 0:NT], mhalf[:, :], -2.0, tg[:, 1:2], ALU.mult, ALU.mult).then_inc(route, 1)
            dve.wait_ge(route, 13)
            dve.tensor_tensor(comb[:, NT:].rearrange("p (e t) -> p t e", t=NT), rp[:, :, :], keep[:, :, :], ALU.mult).then_inc(route, 1)
            dve.wait_ge(route, 14)
            for n in range(2 * JS):
                gate_hidden(n, n)
                if n >= 1:
                    split_hid(n - 1, n - 1)
                if n % 2 == 0:
                    split_w(JS + n // 2, n // 2, (JS + n // 2) % RS)

            def expert(e, last):
                base = e * 8 + 2 * JS
                for u in range(2 * JE):
                    gate_hidden(base + u, u)
                    split_hid(base + u - 1, u - 1 + 2 * JE)
                    if u < 2:
                        add_expert(e, u)
                    if u % 2 == 0 and not (last and u >= JE):
                        i = JS + u // 2 + 2
                        split_w(e * JE + i, (i + JS) % WS, i % RS)

            with dve.Fori(0, NE - 1) as e:
                expert(e, False)
            expert(NE - 1, True)
            split_hid(2 * NM - 1, 2 * JE - 1)
            for c in range(NC):
                add_expert(NE, c)

        @block.gpsimd
        def _(pool):
            def split_wq(g, s):
                pool.wait_ge(wq_hi, g + 1)
                pool.tensor_tensor(w_lo[:, s, 0:2 * D], raw_kvq[:, s, 2 * HD:KVQ], w_hi[:, s, 0:2 * D].bitcast(F32),
                                   ALU.subtract).then_inc(wq_lo, 1)

            def normal_p(b, par):
                pool.wait_ge(rden_ok, b * TPB + par + 1)
                pool.tensor_tensor(by_head(probs[:, par, :]), by_head(probs[:, par, :]),
                                   rden[:, par, :].unsqueeze(2).to_broadcast([P, NH, S]), ALU.mult).then_inc(p_ok, 1)

            for s in range(2):
                split_wq(s, s)
            pool.wait_ge(mhalf_ok, 1)
            pool.wait_ge(vare_ok, 1)
            pool.tensor_tensor(rstd[:, :], vare[:, :], mhalf[:, :], ALU.pow).then_inc(rstd_ok, 1)
            with pool.Fori(1, NG // 2) as it:
                for s in range(2):
                    split_wq(it * 2 + s, s)
            normal_p(0, 0)
            normal_p(0, 1)
            with pool.Fori(1, NB - 1) as b:
                for par in range(TPB):
                    normal_p(b, par)
            for h in range(2):
                if h == 1:
                    for par in range(TPB):
                        normal_p(NB - 1, par)
                o = slice(h * NT // 2, (h + 1) * NT // 2)
                pool.wait_ge(vare2_ok, h + 1)
                pool.tensor_tensor(rstd2[:, o], vare2[:, o], mhalf[:, o], ALU.pow).then_inc(rstd2_ok, 1)


def kernel(x, ctx_1024, mask_BxS2_bf1, g_xattn, g_ffn, L0_xattn_Wq, L0_xattn_Wk, L0_xattn_Wv, L0_xattn_Wo,
           L0_ffn_gate_w, L0_ffn_w1, L0_ffn_w3, L0_ffn_w2, L0_ffn_sw1, L0_ffn_sw3, L0_ffn_sw2):
    import numpy as np
    import concourse.bacc as bacc
    from concourse import mybir as _mybir
    from concourse.bass_utils import run_bass_kernel_spmd

    a = np.asarray
    kv = [a(w).reshape(DV, NG, HD).transpose(1, 0, 2) for w in (L0_xattn_Wk, L0_xattn_Wv)]
    wqT = a(L0_xattn_Wq).reshape(D, NG, 2, HD).transpose(1, 3, 2, 0).reshape(NG, HD, 2 * D)
    wo = a(L0_xattn_Wo).reshape(NG, 2, HD, D).transpose(0, 2, 1, 3).reshape(NG, HD, 2 * D)

    def hidden_tiles(w1, w3, w2):
        n = w1.shape[0] // P
        ups = [w.reshape(n, P, KD, P).transpose(0, 3, 2, 1).reshape(n, P, KD * P) for w in (w1, w3)]
        return np.concatenate(ups + [w2.T.reshape(n, P, D)], axis=2)

    tiles = [hidden_tiles(a(L0_ffn_sw1), a(L0_ffn_sw3), a(L0_ffn_sw2))]
    tiles += [hidden_tiles(a(L0_ffn_w1)[e], a(L0_ffn_w3)[e], a(L0_ffn_w2)[e]) for e in range(NE)]
    e, j = np.meshgrid(np.arange(NE), np.arange(NE), indexing="ij")
    arrays = {
        "x": a(x).reshape(NB * T, D),
        "ctxT": a(ctx_1024).transpose(2, 0, 1).reshape(DV, NB * S),
        "mask": np.broadcast_to(a(mask_BxS2_bf1).view(np.uint8).reshape(1, NB * S), (P, NB * S)),
        "gates": np.broadcast_to(np.concatenate([a(g_xattn), a(g_ffn)]).reshape(1, 2), (P, 2)),
        "kvq": np.concatenate(kv + [wqT], axis=2),
        "wo": wo,
        "gwT": a(L0_ffn_gate_w).reshape(NE, KD, P).transpose(2, 1, 0).reshape(P, KD * NE),
        "ffn": np.concatenate(tiles, axis=0),
        "ident": np.eye(P, dtype=np.float32),
        "before": np.broadcast_to((j < e).astype(np.float32).reshape(1, NE * NE), (P, NE * NE)),
    }
    nc = bacc.Bacc("TRN2", target_bir_lowering=False, num_devices=1)
    feed, args = {}, []
    for name, v in arrays.items():
        v = np.ascontiguousarray(v)
        feed[f"{name}_dram"] = v
        args.append(nc.dram_tensor(f"{name}_dram", v.shape, _mybir.dt.from_np(v.dtype), kind="ExternalInput").ap())
    out = nc.dram_tensor("out_dram", (NB * T, D), F32, kind="ExternalOutput").ap()
    build(nc, *args, out)
    r = run_bass_kernel_spmd(nc, [feed], core_ids=[0])
    return r.results[0]["out_dram"].reshape(NB, T, D)
```

```python
import math
from contextlib import ExitStack

import concourse.bass as bass
from concourse import mybir

F32 = mybir.dt.float32
F32R = mybir.dt.float32r
U8 = mybir.dt.uint8
ALU = mybir.AluOpType
ACT = mybir.ActivationFunctionType
AX = mybir.AxisListType

P = 128
NB, T, D = 4, 256, 256
S, DV = 64, 128
NH, NG, HD = 16, 8, 128
KD = D // P
NT = NB * T // P
TPB = T // P
NE, H, HS = 4, 512, 256
JE, JS = H // P, HS // P
NM = JS + NE * JE
WS = 4
RS = 2
HR = 4
CH = 512
TC = CH // P
NC = NB * T // CH
SW = NH * S
KVQ = 2 * HD + 2 * D
WOC = 2 * D
UPC = 2 * KD * P
FFC = UPC + D
SCALE = float(HD) ** -0.5
EPS = 1e-5
MASKED = 1e30
PARTS = [(0, 4), (4, 6), (6, 8)]
TURN_AFTER = {0: 1, 2: 0, 3: 2}


def wait(eng, sem, n):
    if isinstance(n, int) and n <= 0:
        return
    eng.wait_ge(sem, n)


def build(nc, x, ctxT, mask, gates, kvq, wo, gwT, ffn, ident_c, before_c, out):
    with ExitStack() as ctx:
        def sb(name, shape, dt=F32):
            return ctx.enter_context(nc.sbuf_tensor(name, shape, dt))

        def sem(name):
            return ctx.enter_context(nc.semaphore(name))

        x_sb = sb("x_sb", [P, NT * D])
        A_hi = sb("A_hi", [P, KD, NB, SW], F32R)
        A_lo = sb("A_lo", [P, KD, NB, SW], F32R)
        VO_hi = sb("VO_hi", [P, NB, NG, D], F32R)
        VO_lo = sb("VO_lo", [P, NB, NG, D], F32R)
        xT_hi = sb("xT_hi", [P, KD, NT * P], F32R)
        xT_lo = sb("xT_lo", [P, KD, NT * P], F32R)
        PT_hi = sb("PT_hi", [P, NG, P], F32R)
        PT_lo = sb("PT_lo", [P, NG, P], F32R)
        w_hi = sb("w_hi", [P, WS, FFC], F32R)
        w_lo = sb("w_lo", [P, WS, FFC], F32R)
        raw = sb("raw", [P, RS, FFC])
        probs = sb("probs", [P, TPB, SW])
        xn0 = sb("xn0", [P, TPB, D])
        ident = sb("ident", [P, P])
        before = sb("before", [P, NE * NE])
        mask_u8 = sb("mask_u8", [P, NB * S], U8)
        bias = sb("bias", [P, NB * S], F32R)
        onerow = sb("onerow", [P, P], F32R)
        anyvalid = sb("anyvalid", [P, NB])
        tga = sb("tga", [P, NB])
        gates_sb = sb("gates_sb", [P, 2])
        tg = sb("tg", [P, 2])
        gw_sb = sb("gw_sb", [P, KD * NE])
        gw_hi = sb("gw_hi", [P, KD * NE], F32R)
        gw_lo = sb("gw_lo", [P, KD * NE], F32R)
        stats = sb("stats", [P, NT * 6])
        mv = sb("mv", [P, NT * 2])
        stats2 = sb("stats2", [P, NT * 6])
        mv2 = sb("mv2", [P, NT * 2])
        vare = sb("vare", [P, NT])
        vare2 = sb("vare2", [P, NT])
        rstd = sb("rstd", [P, NT])
        rstd2 = sb("rstd2", [P, NT])
        mhalf = sb("mhalf", [P, NT])
        euler = sb("euler", [P, NT * NE])
        mx = sb("mx", [P, TPB, NH])
        den = sb("den", [P, TPB, NH])
        rcp = sb("rcp", [P, TPB, NH])
        logits = sb("logits", [P, NT, NE])
        lmax = sb("lmax", [P, NT])
        lexp = sb("lexp", [P, NT, NE])
        lsum = sb("lsum", [P, NT])
        lrcp = sb("lrcp", [P, NT])
        rp = sb("rp", [P, NT, NE])
        gt = sb("gt", [P, NT, NE * NE])
        eq = sb("eq", [P, NT, NE * NE])
        rank = sb("rank", [P, NT, NE])
        keep = sb("keep", [P, NT, NE])
        comb = sb("comb", [P, (1 + NE) * NT])

        raw_kvq = raw
        raw_wo = probs[:, 0, :].rearrange("p (s n) -> p s n", s=2)
        VT = probs[:, 1, 0:2 * NB * S].rearrange("p (s n) -> p s n", s=2)
        ctx_sb = probs[:, 1, 2 * NB * S:3 * NB * S]
        KT_hi = PT_hi[:, 0:4, :].rearrange("p (s a) n -> p s (a n)", s=2)
        KT_lo = PT_lo[:, 0:4, :].rearrange("p (s a) n -> p s (a n)", s=2)
        mask_f = xn0[:, 0, :]
        xn1 = probs[:, 1, 0:TPB * D].rearrange("p (t d) -> p t d", d=D)
        xn = [xn0, xn0, xn0, xn1]
        hid_hi = A_hi[:, 0, 0:HR * CH // SW, :].rearrange("p a (b n) -> p (a b) n", n=CH)
        hid_lo = A_lo[:, 0, 0:HR * CH // SW, :].rearrange("p a (b n) -> p (a b) n", n=CH)
        hid_f = probs[:, 0, :].rearrange("p (s n) -> p s n", s=2)

        bankP, bankQ, bankR, bankS = [ctx.enter_context(nc.psum_tensor(f"bank{c}", [P, 2, 512], F32)) for c in "PQRS"]
        scores_ps = [bankP, bankQ]
        up_ps = [bankP, bankQ]
        acc_ps = [bankR, bankS]

        ctx_ld, x_ld, const_ld = sem("ctx_ld"), sem("x_ld"), sem("const_ld")
        kvq_ld = [sem(f"kvq_ld{i}") for i in range(2)]
        wo_ld = [sem(f"wo_ld{i}") for i in range(2)]
        ffn_ld = [sem(f"ffn_ld{i}") for i in range(RS)]
        prep = sem("prep")
        onerow_ok, tg_ok = sem("onerow_ok"), sem("tg_ok")
        gwhi_ok, gwlo_ok = sem("gwhi_ok"), sem("gwlo_ok")
        kv_ps, k_hi, kv_sb = sem("kv_ps"), sem("k_hi"), sem("kv_sb")
        wq_hi, wq_lo = sem("wq_hi"), sem("wq_lo")
        a_ps, a_hi, a_lo = sem("a_ps"), sem("a_hi"), sem("a_lo")
        vo_ps, vo_hi, vo_lo = sem("vo_ps"), sem("vo_hi"), sem("vo_lo")
        st1, mv_ok, bias_ok, vare_ok, rstd_ok, mhalf_ok = sem("st1"), sem("mv_ok"), sem("bias_ok"), sem("vare_ok"), sem("rstd_ok"), sem("mhalf_ok")
        xn_ok, xt_ps, xt_hi, xt_lo = sem("xn_ok"), sem("xt_ps"), sem("xt_hi"), sem("xt_lo")
        sc_ps, mx_ok, sub_ok, exp_ok = sem("sc_ps"), sem("mx_ok"), sem("sub_ok"), sem("exp_ok")
        den_ok, rcp_ok, p_ok = sem("den_ok"), sem("rcp_ok"), sem("p_ok")
        pt_ps, pt_hi, pt_lo = sem("pt_ps"), sem("pt_hi"), sem("pt_lo")
        pv_ps, x1_ok, st2, mv2_ok = sem("pv_ps"), sem("x1_ok"), sem("st2"), sem("mv2_ok")
        vare2_ok, rstd2_ok = sem("vare2_ok"), sem("rstd2_ok")
        xn2_ok, x2_ps, x2_hi, x2_lo = ([sem(f"{n}{c}") for c in range(NT // TPB)] for n in ("xn2_ok", "x2_ps", "x2_hi", "x2_lo"))
        lg_ps, route, lexp_ok = sem("lg_ps"), sem("route"), sem("lexp_ok")
        wf_hi, wf_lo = sem("wf_hi"), sem("wf_lo")
        u_ps, g_ps, silu_ok, hid_ok = sem("u_ps"), sem("g_ps"), sem("silu_ok"), sem("hid_ok")
        hid_hi_ok, hid_lo_ok = sem("hid_hi_ok"), sem("hid_lo_ok")
        down_ps, y_ok, out_ok, stored = sem("down_ps"), sem("y_ok"), sem("out_ok"), sem("stored")

        def split3(eng, acc, l_hi, l_lo, r_hi, r_lo, start, stop, **kw):
            eng.matmul(acc, l_hi, r_hi, start=start, stop=False, **kw)
            eng.matmul(acc, l_hi, r_lo, start=False, stop=False, **kw)
            return eng.matmul(acc, l_lo, r_hi, start=False, stop=stop, **kw)

        def by_head(ap):
            return ap.rearrange("p (h s) -> p h s", s=S)

        def xtile(n):
            return x_sb[:, bass.ds(n * D, D)]

        block = ctx.enter_context(nc.Block())

        @block.sync
        def _(sp):
            def load_head(g, s, n):
                wait(sp, kv_ps, g - 1)
                wait(sp, wq_lo, g - 1)
                sp.dma_start(raw_kvq[:, s, :], kvq[bass.ds(g, 1), :, :].rearrange("g p n -> p (g n)")).then_inc(kvq_ld[s], 16)
                wait(sp, vo_ps, (g - 1) * 2)
                sp.dma_start(raw_wo[:, s, :], wo[bass.ds(g, 1), :, :].rearrange("g p n -> p (g n)")).then_inc(wo_ld[s], 16)

            def load_ffn(m, s):
                wait(sp, wf_lo, m - RS + 1)
                sp.dma_start(raw[:, s, :], ffn[bass.ds(m, 1), :, :].rearrange("g p n -> p (g n)")).then_inc(ffn_ld[s], 16)

            sp.dma_start(ctx_sb[:, :], ctxT).then_inc(ctx_ld, 16)
            load_head(0, 0, 0)
            load_head(1, 1, 0)
            sp.dma_start(x_sb[:, :].rearrange("p (t d) -> p t d", d=D), x.rearrange("(t p) d -> p t d", p=P)).then_inc(x_ld, 16)
            sp.dma_start(gates_sb[:, :], gates).then_inc(const_ld, 16)
            sp.dma_start(mask_u8[:, :], mask).then_inc(const_ld, 16)
            sp.dma_start(ident[:, :], ident_c).then_inc(const_ld, 16)
            sp.dma_start(before[:, :], before_c).then_inc(const_ld, 16)
            sp.dma_start(gw_sb[:, :], gwT).then_inc(const_ld, 16)
            with sp.Fori(1, NG // 2) as it:
                for s in range(2):
                    load_head(it * 2 + s, s, it)
            sp.wait_ge(wq_lo, NG)
            sp.wait_ge(vo_ps, 2 * NG)
            for s in range(RS):
                load_ffn(s, s)
            with sp.Fori(1, NM // RS) as it:
                for s in range(RS):
                    load_ffn(it * RS + s, s)
            for t in range(NT):
                sp.wait_ge(out_ok, t + 1)
                sp.dma_start(out.rearrange("(t p) d -> t p d", p=P)[t], x_sb[:, t * D:(t + 1) * D]).then_inc(stored, 16)
            sp.wait_ge(stored, 16 * NT)

        @block.tensor
        def _(pe):
            def keys_values(g, s, n):
                pe.wait_ge(kvq_ld[s], (n + 1) * 16)
                wait(pe, kv_sb, g - 1)
                pe.matmul(bankP[:, s, 0:NB * S], raw_kvq[:, s, 0:HD], ctx_sb[:, :], start=True, stop=True)
                pe.matmul(bankP[:, s, NB * S:], raw_kvq[:, s, HD:2 * HD], ctx_sb[:, :], start=True, stop=True).then_inc(kv_ps, 1)

            def query_side(g, s):
                pe.wait_ge(kv_sb, g + 1)
                pe.wait_ge(wq_lo, g + 1)
                for hh in range(2):
                    wait(pe, a_lo, (g - 1) * 2 + hh + 1)
                    for k in range(KD):
                        c = hh * D + k * P
                        mm = split3(pe, bankQ[:, hh, k * D:(k + 1) * D], w_hi[:, s, c:c + P], w_lo[:, s, c:c + P],
                                    KT_hi[:, s, :], KT_lo[:, s, :], True, True)
                    mm.then_inc(a_ps, 1)

            def output_side(g, s, n):
                pe.wait_ge(wo_ld[s], (n + 1) * 16)
                for pair in range(2):
                    wait(pe, vo_lo, (g - 1) * 2 + pair + 1)
                    for r in range(2):
                        b = pair * 2 + r
                        for hh in range(2):
                            mm = pe.matmul(bankR[hh * S:(hh + 1) * S, pair, r * D:(r + 1) * D], VT[:, s, b * S:(b + 1) * S],
                                           raw_wo[:, s, hh * D:(hh + 1) * D], start=True, stop=True)
                    mm.then_inc(vo_ps, 1)

            def heads(it):
                g = it * 2
                keys_values(g + 1, 1, it)
                query_side(g, 0)
                output_side(g, 0, it)
                keys_values(g + 2, 0, it + 1)
                query_side(g + 1, 1)
                output_side(g + 1, 1, it)

            def turn_x(b):
                pe.wait_ge(xn_ok, b + 1)
                wait(pe, xt_lo, b)
                for par in range(TPB):
                    for k in range(KD):
                        c = (par * KD + k) * P
                        mm = pe.transpose(bankS[:, 0, c:c + P], xn0[:, par, k * P:(k + 1) * P], ident[:, :])
                mm.then_inc(xt_ps, 1)

            def scores(b, par):
                n = b * TPB + par
                pe.wait_ge(xt_lo, b + 1)
                wait(pe, sub_ok, n - 1)
                for hf in range(2):
                    acc = scores_ps[par][:, hf, :]
                    pe.matmul(acc, onerow[:, :], bias[:, bass.ds(b * S, S)].unsqueeze(1).to_broadcast([P, NH // 2, S]),
                              start=True, stop=False)
                    for k in range(KD):
                        mm = split3(pe, acc, xT_hi[:, k, par * P:(par + 1) * P], xT_lo[:, k, par * P:(par + 1) * P],
                                    A_hi[:, k, bass.ds(b, 1), hf * 512:(hf + 1) * 512].rearrange("p a n -> p (a n)"),
                                    A_lo[:, k, bass.ds(b, 1), hf * 512:(hf + 1) * 512].rearrange("p a n -> p (a n)"),
                                    False, k == KD - 1)
                mm.then_inc(sc_ps, 1)

            def turn_p(b, par):
                n = b * TPB + par
                pe.wait_ge(p_ok, n + 1)
                for q in range(2):
                    for g in range(NG // 2):
                        c = (q * NG // 2 + g) * P
                        mm = pe.transpose(bankR[:, q, g * P:(g + 1) * P], probs[:, par, c:c + P], ident[:, :])
                    mm.then_inc(pt_ps, 1)

            def attend(b, par):
                n = b * TPB + par
                for g in range(NG):
                    if g % (NG // 2) == 0:
                        pe.wait_ge(pt_lo, n * 2 + g // (NG // 2) + 1)
                    mm = split3(pe, bankS[:, 1, 0:D], PT_hi[:, g, :], PT_lo[:, g, :],
                                VO_hi[:, bass.ds(b, 1), g, :].rearrange("p a n -> p (a n)"),
                                VO_lo[:, bass.ds(b, 1), g, :].rearrange("p a n -> p (a n)"), g == 0, g == NG - 1)
                mm.then_inc(pv_ps, 1)

            def attend_batch(b):
                turn_p(b - 1, 0)
                scores(b, 0)
                attend(b - 1, 0)
                turn_p(b - 1, 1)
                scores(b, 1)
                turn_x(b + 1)
                attend(b - 1, 1)

            def turn_x2(c):
                pe.wait_ge(xn2_ok[c], 1)
                if c in TURN_AFTER:
                    pe.wait_ge(x2_lo[TURN_AFTER[c]], 1)
                for par in range(TPB):
                    for k in range(KD):
                        o = (par * KD + k) * P
                        mm = pe.transpose(bankS[:, 0, o:o + P], xn[c][:, par, k * P:(k + 1) * P], ident[:, :])
                mm.then_inc(x2_ps[c], 1)

            def route_tiles(t0, t1):
                for t in range(t0, t1):
                    for k in range(KD):
                        l_hi, l_lo = (w[:, k, t * P:(t + 1) * P] for w in (xT_hi, xT_lo))
                        r_hi, r_lo = (w[:, k * NE:(k + 1) * NE] for w in (gw_hi, gw_lo))
                        split3(pe, bankS[:, 1, t * NE:(t + 1) * NE], l_hi, l_lo, r_hi, r_lo, k == 0, False)
                        mm = pe.matmul(bankS[:, 1, t * NE:(t + 1) * NE], l_lo, r_lo, start=False, stop=k == KD - 1)
                return mm

            def up_unit(u, s, c):
                for mat, done in ((0, u_ps), (1, g_ps)):
                    for k in range(KD):
                        o = (mat * KD + k) * P
                        mm = split3(pe, up_ps[u % 2][:, mat, :], w_hi[:, s, o:o + P], w_lo[:, s, o:o + P],
                                    xT_hi[:, k, c * CH:(c + 1) * CH], xT_lo[:, k, c * CH:(c + 1) * CH], k == 0, k == KD - 1)
                    mm.then_inc(done, 1)

            def down_unit(n, u, s, c, first, last, e):
                pe.wait_ge(hid_lo_ok, n + 1)
                if first:
                    wait(pe, y_ok, (e - 1) * NC + c + 1)
                for tt in range(TC):
                    o = tt * P
                    mm = split3(pe, acc_ps[c][:, tt // 2, tt % 2 * D:(tt % 2 + 1) * D],
                                hid_hi[:, u % HR, o:o + P], hid_lo[:, u % HR, o:o + P],
                                w_hi[:, s, UPC:FFC], w_lo[:, s, UPC:FFC],
                                first and tt % 2 == 0, last, skip_group_check=True)
                mm.then_inc(down_ps, 1)

            pe.wait_ge(ctx_ld, 16)
            keys_values(0, 0, 0)
            heads(0)
            with pe.Fori(1, NG // 2 - 1) as it:
                heads(it)
            pe.wait_ge(const_ld, 80)
            it = NG // 2 - 1
            keys_values(NG - 1, 1, it)
            query_side(NG - 2, 0)
            output_side(NG - 2, 0, it)
            query_side(NG - 1, 1)
            turn_x(0)
            output_side(NG - 1, 1, it)
            pe.wait_ge(onerow_ok, 1)
            pe.wait_ge(bias_ok, 1)
            pe.wait_ge(kv_sb, NG)
            pe.wait_ge(a_lo, 2 * NG)
            scores(0, 0)
            scores(0, 1)
            turn_x(1)
            pe.wait_ge(vo_lo, 2 * NG)
            with pe.Fori(1, NB - 1) as b:
                attend_batch(b)
            b = NB - 1
            turn_p(b - 1, 0)
            scores(b, 0)
            attend(b - 1, 0)
            turn_x2(1)
            turn_p(b - 1, 1)
            scores(b, 1)
            turn_x2(0)
            attend(b - 1, 1)
            turn_p(b, 0)
            pe.wait_ge(wf_lo, 1)
            pe.wait_ge(sub_ok, NT - 1)
            pe.wait_ge(x2_lo[0], 1)
            up_unit(0, JS, 0)
            attend(b, 0)
            turn_p(b, 1)
            turn_x2(2)
            pe.wait_ge(wf_lo, 2)
            pe.wait_ge(sub_ok, NT)
            up_unit(1, JS + 1, 0)
            attend(b, 1)
            down_unit(0, 0, JS, 0, True, False, 0)
            pe.wait_ge(gwlo_ok, 1)
            pe.wait_ge(x2_lo[2], 1)
            pe.wait_ge(x1_ok, NT)
            route_tiles(0, NT - 2)
            down_unit(1, 1, JS + 1, 0, False, True, 0)
            turn_x2(3)
            pe.wait_ge(x2_lo[3], 1)
            route_tiles(NT - 2, NT).then_inc(lg_ps, 1)
            for n in (2, 3):
                pe.wait_ge(hid_ok, n - 1)
                up_unit(n, JS + n - 2, 1)
            pe.wait_ge(route, 1)

            def expert(e, first):
                base = e * 8 + 2 * JS
                for u in range(2 * JE):
                    n = base + u
                    pe.wait_ge(wf_lo, e * JE + JS + u // 2 + 1)
                    pe.wait_ge(hid_ok, n - 1)
                    up_unit(u, u // 2, u % 2)
                    if u >= 2:
                        down_unit(n - 2, u - 2, u // 2 - 1, u % 2, u < 4, False, e + 1)
                    elif first:
                        down_unit(n - 2, u + 2, JS + u, 1, u == 0, u == 1, 0)
                    else:
                        down_unit(n - 2, u + 2 * JE - 2, WS - 1, u, False, True, e)

            expert(0, True)
            with pe.Fori(1, NE) as e:
                expert(e, False)
            for u in range(2):
                n = 2 * NM - 2 + u
                down_unit(n, u + 2 * JE - 2, WS - 1, u, False, True, NE)

        @block.scalar
        def _(act):
            def split_wq(g, s, n):
                act.wait_ge(kvq_ld[s], (n + 1) * 16)
                wait(act, a_ps, (g - 1) * 2)
                act.copy(w_hi[:, s, 0:2 * D], raw_kvq[:, s, 2 * HD:KVQ]).then_inc(wq_hi, 1)

            def split_k(g, s):
                act.wait_ge(kv_ps, g + 1)
                act.copy(KT_hi[:, s, :], bankP[:, s, 0:NB * S]).then_inc(k_hi, 1)

            def evict_query_side(g):
                for hh in range(2):
                    act.wait_ge(a_ps, g * 2 + hh + 1)
                    act.copy(A_hi[:, :, :, bass.ds(g * 2 * S + hh * S, S)],
                             bankQ[:, hh, :].rearrange("p (k b s) -> p k b s", k=KD, b=NB)).then_inc(a_hi, 1)

            def evict_output_side(g):
                for pair in range(2):
                    act.wait_ge(vo_ps, g * 2 + pair + 1)
                    act.copy(VO_hi[:, pair * 2:pair * 2 + 2, bass.ds(g, 1), :].rearrange("p b a n -> p b (a n)"),
                             bankR[:, pair, :].rearrange("p (b n) -> p b n", b=2)).then_inc(vo_hi, 1)

            def heads(it):
                g = it * 2
                split_wq(g + 1, 1, it)
                split_k(g + 1, 1)
                evict_query_side(g)
                evict_output_side(g)
                split_wq(g + 2, 0, it + 1)
                split_k(g + 2, 0)
                evict_query_side(g + 1)
                evict_output_side(g + 1)

            def split_x(b):
                act.wait_ge(xt_ps, b + 1)
                wait(act, sc_ps, b * TPB)
                act.copy(xT_hi[:, :, 0:TPB * P].rearrange("p k (t n) -> p t k n", n=P),
                         bankS[:, 0, :].rearrange("p (t k n) -> p t k n", t=TPB, k=KD)).then_inc(xt_hi, 1)

            def exponent(b, par):
                act.wait_ge(sub_ok, b * TPB + par + 1)
                act.activation(probs[:, par, :], probs[:, par, :], ACT.Exp, scale=SCALE).then_inc(exp_ok, 1)

            def split_p(b, par):
                n = b * TPB + par
                for q in range(2):
                    act.wait_ge(pt_ps, n * 2 + q + 1)
                    act.copy(PT_hi[:, q * NG // 2:(q + 1) * NG // 2, :],
                             bankR[:, q, :].rearrange("p (g n) -> p g n", n=P)).then_inc(pt_hi, 1)

            def attend_batch(b):
                split_p(b - 1, 0)
                exponent(b, 0)
                split_p(b - 1, 1)
                split_x(b + 1)
                exponent(b, 1)

            def split_x2(c):
                act.wait_ge(x2_ps[c], 1)
                act.copy(xT_hi[:, :, c * TPB * P:(c + 1) * TPB * P].rearrange("p k (t n) -> p t k n", n=P),
                         bankS[:, 0, :].rearrange("p (t k n) -> p t k n", t=TPB, k=KD)).then_inc(x2_hi[c], 1)

            def split_w(m, s, r, n):
                act.wait_ge(ffn_ld[r], (n + 1) * 16)
                wait(act, down_ps, 3 if isinstance(m, int) and m == WS else (m - WS) * 2 + 2)
                act.copy(w_hi[:, s, :], raw[:, r, :]).then_inc(wf_hi, 1)

            def silu(n, u):
                act.wait_ge(u_ps, n + 1)
                wait(act, hid_lo_ok, n - 1)
                act.activation(hid_f[:, u % 2, :], up_ps[u % 2][:, 0, :], ACT.Silu).then_inc(silu_ok, 1)

            def split_hid(n, u):
                act.wait_ge(hid_ok, n + 1)
                wait(act, down_ps, n - HR + 1)
                act.copy(hid_hi[:, u % HR, :], hid_f[:, u % 2, :]).then_inc(hid_hi_ok, 1)

            split_wq(0, 0, 0)
            split_k(0, 0)
            heads(0)
            act.wait_ge(const_ld, 80)
            act.activation(tg[:, :], gates_sb[:, :], ACT.Tanh).then_inc(tg_ok, 1)
            act.copy(gw_hi[:, :], gw_sb[:, :]).then_inc(gwhi_ok, 1)
            with act.Fori(1, NG // 2 - 1) as it:
                heads(it)
            split_wq(NG - 1, 1, NG // 2 - 1)
            split_k(NG - 1, 1)
            evict_query_side(NG - 2)
            evict_output_side(NG - 2)
            evict_query_side(NG - 1)
            split_x(0)
            evict_output_side(NG - 1)
            exponent(0, 0)
            exponent(0, 1)
            split_x(1)
            for m in range(JS):
                split_w(m, JS + m, m % RS, m // RS)
            with act.Fori(1, NB - 1) as b:
                attend_batch(b)
            b = NB - 1
            split_p(b - 1, 0)
            exponent(b, 0)
            split_x2(1)
            split_p(b - 1, 1)
            split_x2(0)
            exponent(b, 1)
            split_p(b, 0)
            silu(0, 0)
            split_hid(0, 0)
            split_p(b, 1)
            split_x2(2)
            silu(1, 1)
            split_hid(1, 1)
            split_x2(3)
            for m in (JS, JS + 1):
                split_w(m, m - JS, m % RS, m // RS)
            silu(2, 2)
            silu(3, 3)
            split_hid(2, 2)

            def expert(e, last):
                base = e * 8 + 2 * JS
                for u in range(2 * JE):
                    silu(base + u, u)
                    split_hid(base + u - 1, u - 1 + 2 * JE)
                    if u % 2 == 0 and not (last and u >= JE):
                        i = JS + u // 2 + 2
                        split_w(e * JE + i, (i + JS) % WS, i % RS, e * (JE // RS) + i // RS)

            expert(0, False)
            with act.Fori(1, NE - 1) as e:
                expert(e, False)
            expert(NE - 1, True)
            split_hid(2 * NM - 1, 2 * JE - 1)

        @block.vector
        def _(dve):
            def split_kv(g, s):
                dve.wait_ge(k_hi, g + 1)
                dve.tensor_tensor(KT_lo[:, s, :], bankP[:, s, 0:NB * S], KT_hi[:, s, :].bitcast(F32), ALU.subtract)
                wait(dve, vo_ps, (g - 1) * 2)
                dve.tensor_copy(VT[:, s, :], bankP[:, s, NB * S:]).then_inc(kv_sb, 1)

            def evict_query_side(g):
                for hh in range(2):
                    dve.wait_ge(a_hi, g * 2 + hh + 1)
                    o = bass.ds(g * 2 * S + hh * S, S)
                    dve.tensor_tensor(A_lo[:, :, :, o], bankQ[:, hh, :].rearrange("p (k b s) -> p k b s", k=KD, b=NB),
                                      A_hi[:, :, :, o].bitcast(F32), ALU.subtract).then_inc(a_lo, 1)

            def evict_output_side(g):
                for pair in range(2):
                    dve.wait_ge(vo_hi, g * 2 + pair + 1)
                    dve.tensor_tensor(VO_lo[:, pair * 2:pair * 2 + 2, bass.ds(g, 1), :].rearrange("p b a n -> p b (a n)"),
                                      bankR[:, pair, :].rearrange("p (b n) -> p b n", b=2),
                                      VO_hi[:, pair * 2:pair * 2 + 2, bass.ds(g, 1), :].rearrange("p b a n -> p b (a n)").bitcast(F32),
                                      ALU.subtract).then_inc(vo_lo, 1)

            def heads(it):
                g = it * 2
                split_kv(g + 1, 1)
                evict_query_side(g)
                evict_output_side(g)
                split_kv(g + 2, 0)
                evict_query_side(g + 1)
                evict_output_side(g + 1)

            def normal_x(b):
                wait(dve, xt_ps, b)
                for par in range(TPB):
                    n = b * TPB + par
                    ins = dve.tensor_scalar(xn0[:, par, :], xtile(n), mv[:, bass.ds(n * 2, 1)], rstd[:, bass.ds(n, 1)],
                                            ALU.subtract, ALU.mult)
                ins.then_inc(xn_ok, 1)

            def split_x(b):
                dve.wait_ge(xt_hi, b + 1)
                for par in range(TPB):
                    o = slice(par * P, (par + 1) * P)
                    ins = dve.tensor_tensor(xT_lo[:, :, o], bankS[:, 0, par * D:(par + 1) * D].rearrange("p (k n) -> p k n", k=KD),
                                            xT_hi[:, :, o].bitcast(F32), ALU.subtract)
                ins.then_inc(xt_lo, 1)

            def less_max(b, par):
                n = b * TPB + par
                dve.wait_ge(sc_ps, n + 1)
                sc = scores_ps[par][:, :, :].rearrange("p a (h s) -> p (a h) s", s=S)
                dve.tensor_reduce(mx[:, par, :], sc, AX.X, ALU.max).then_inc(mx_ok, 1)
                dve.wait_ge(mx_ok, n + 1)
                wait(dve, pt_ps, (n - 1) * 2)
                dve.tensor_tensor(by_head(probs[:, par, :]), sc, mx[:, par, :].unsqueeze(2).to_broadcast([P, NH, S]),
                                  ALU.subtract).then_inc(sub_ok, 1)

            def denominator(b, par):
                n = b * TPB + par
                dve.wait_ge(exp_ok, n + 1)
                wait(dve, p_ok, n - 1)
                dve.tensor_reduce(den[:, par, :], by_head(probs[:, par, :]), AX.X, ALU.add).then_inc(den_ok, 1)
                dve.wait_ge(den_ok, n + 1)
                dve.reciprocal(rcp[:, par, :], den[:, par, :]).then_inc(rcp_ok, 1)

            def split_p(b, par):
                n = b * TPB + par
                for q in range(2):
                    dve.wait_ge(pt_hi, n * 2 + q + 1)
                    o = slice(q * NG // 2, (q + 1) * NG // 2)
                    dve.tensor_tensor(PT_lo[:, o, :], bankR[:, q, :].rearrange("p (g n) -> p g n", n=P),
                                      PT_hi[:, o, :].bitcast(F32), ALU.subtract).then_inc(pt_lo, 1)

            def add_attention(b, par):
                n = b * TPB + par
                dve.wait_ge(pv_ps, n + 1)
                dve.scalar_tensor_tensor(xtile(n), bankS[:, 1, 0:D], tga[:, bass.ds(b, 1)], xtile(n), ALU.mult, ALU.add).then_inc(x1_ok, 1)
                dve.wait_ge(x1_ok, n + 1)
                dve.bn_stats(stats2[:, bass.ds(n * 6, 6)], xtile(n)).then_inc(st2, 1)

            def attend_batch(b):
                split_p(b - 1, 0)
                less_max(b, 0)
                add_attention(b - 1, 0)
                denominator(b, 0)
                normal_x(b + 1)
                split_p(b - 1, 1)
                less_max(b, 1)
                split_x(b + 1)
                add_attention(b - 1, 1)
                denominator(b, 1)

            def variance2(h):
                t0, t1 = PARTS[h]
                dve.wait_ge(st2, t1)
                for n in range(t0, t1):
                    dve.bn_aggr(mv2[:, n * 2:n * 2 + 2], stats2[:, n * 6:n * 6 + 6]).then_inc(mv2_ok, 1)
                dve.wait_ge(mv2_ok, t1)
                dve.tensor_scalar(vare2[:, t0:t1], mv2[:, :].rearrange("p (t c) -> p t c", c=2)[:, t0:t1, 1], EPS, None,
                                  ALU.add).then_inc(vare2_ok, 1)

            def normal_x2(c):
                dve.wait_ge(rstd2_ok, max(c, 1))
                if c in TURN_AFTER:
                    dve.wait_ge(x2_ps[TURN_AFTER[c]], 1)
                for par in range(TPB):
                    n = c * TPB + par
                    ins = dve.tensor_scalar(xn[c][:, par, :], xtile(n), mv2[:, n * 2:n * 2 + 1], rstd2[:, n:n + 1],
                                            ALU.subtract, ALU.mult)
                ins.then_inc(xn2_ok[c], 1)

            def split_x2(c):
                dve.wait_ge(x2_hi[c], 1)
                o = slice(c * TPB * P, (c + 1) * TPB * P)
                dve.tensor_tensor(xT_lo[:, :, o].rearrange("p k (t n) -> p t k n", n=P),
                                  bankS[:, 0, :].rearrange("p (t k n) -> p t k n", t=TPB, k=KD),
                                  xT_hi[:, :, o].rearrange("p k (t n) -> p t k n", n=P).bitcast(F32),
                                  ALU.subtract).then_inc(x2_lo[c], 1)

            def split_w(m, s, r):
                dve.wait_ge(wf_hi, m + 1)
                dve.tensor_tensor(w_lo[:, s, :], raw[:, r, :], w_hi[:, s, :].bitcast(F32), ALU.subtract).then_inc(wf_lo, 1)

            def gate_hidden(n, u):
                dve.wait_ge(silu_ok, n + 1)
                dve.wait_ge(g_ps, n + 1)
                dve.tensor_tensor(hid_f[:, u % 2, :], up_ps[u % 2][:, 1, :], hid_f[:, u % 2, :], ALU.mult).then_inc(hid_ok, 1)

            def split_hid(n, u):
                dve.wait_ge(hid_hi_ok, n + 1)
                dve.tensor_tensor(hid_lo[:, u % HR, :], hid_f[:, u % 2, :], hid_hi[:, u % HR, :].bitcast(F32),
                                  ALU.subtract).then_inc(hid_lo_ok, 1)

            def add_expert(e, c, final=False):
                dve.wait_ge(down_ps, JS if isinstance(e, int) and e == 0 and c == 0 else e * 8 + 2 * JS - 1 + c)
                for tt in range(TC):
                    t = c * TC + tt
                    ins = dve.scalar_tensor_tensor(x_sb[:, t * D:(t + 1) * D], acc_ps[c][:, tt // 2, tt % 2 * D:(tt % 2 + 1) * D],
                                                   comb[:, bass.ds(e * NT + t, 1)], x_sb[:, t * D:(t + 1) * D], ALU.mult, ALU.add)
                    if final:
                        ins.then_inc(out_ok, 1)
                if not final:
                    ins.then_inc(y_ok, 1)

            dve.memset(onerow[:, :].bitcast(F32), 0.0).then_inc(prep, 1)
            dve.wait_ge(prep, 1)
            dve.memset(onerow[0:1, :].bitcast(F32), 1.0).then_inc(onerow_ok, 1)
            dve.memset(mhalf[:, :], -0.5)
            dve.memset(euler[:, :], math.e).then_inc(mhalf_ok, 1)
            split_kv(0, 0)
            heads(0)
            dve.wait_ge(x_ld, 16)
            for n in range(NT // 2):
                dve.bn_stats(stats[:, n * 6:n * 6 + 6], xtile(n)).then_inc(st1, 1)
            with dve.Fori(1, NG // 2 - 1) as it:
                heads(it)
                for i in range(NT // 4):
                    n = it * (NT // 4) + i + NT // 4
                    dve.bn_stats(stats[:, bass.ds(n * 6, 6)], xtile(n)).then_inc(st1, 1)
            dve.wait_ge(st1, NT)
            for n in range(NT):
                dve.bn_aggr(mv[:, n * 2:n * 2 + 2], stats[:, n * 6:n * 6 + 6]).then_inc(mv_ok, 1)
            dve.wait_ge(mv_ok, NT)
            dve.tensor_scalar(vare[:, :], mv[:, :].rearrange("p (t c) -> p t c", c=2)[:, :, 1], EPS, None, ALU.add).then_inc(vare_ok, 1)
            dve.wait_ge(const_ld, 80)
            dve.tensor_copy(mask_f[:, :], mask_u8[:, :]).then_inc(prep, 1)
            dve.wait_ge(prep, 2)
            dve.tensor_scalar(bias[:, :], mask_f[:, :], -1.0, MASKED, ALU.add, ALU.mult).then_inc(bias_ok, 1)
            dve.tensor_reduce(anyvalid[:, :], mask_f[:, :].rearrange("p (b s) -> p b s", s=S), AX.X, ALU.max).then_inc(prep, 1)
            dve.wait_ge(prep, 3)
            dve.wait_ge(tg_ok, 1)
            dve.tensor_scalar(tga[:, :], anyvalid[:, :], tg[:, 0:1], None, ALU.mult)
            dve.tensor_scalar(comb[:, 0:NT], mhalf[:, :], -2.0, tg[:, 1:2], ALU.mult, ALU.mult)
            dve.wait_ge(gwhi_ok, 1)
            dve.tensor_tensor(gw_lo[:, :], gw_sb[:, :], gw_hi[:, :].bitcast(F32), ALU.subtract).then_inc(gwlo_ok, 1)
            split_kv(NG - 1, 1)
            evict_query_side(NG - 2)
            evict_output_side(NG - 2)
            dve.wait_ge(rstd_ok, 1)
            normal_x(0)
            evict_query_side(NG - 1)
            split_x(0)
            evict_output_side(NG - 1)
            less_max(0, 0)
            normal_x(1)
            denominator(0, 0)
            less_max(0, 1)
            split_x(1)
            denominator(0, 1)
            for m in range(JS):
                split_w(m, JS + m, m % RS)
            with dve.Fori(1, NB - 1) as b:
                attend_batch(b)
            b = NB - 1
            variance2(0)
            split_p(b - 1, 0)
            less_max(b, 0)
            normal_x2(1)
            add_attention(b - 1, 0)
            denominator(b, 0)
            split_p(b - 1, 1)
            split_x2(1)
            normal_x2(0)
            less_max(b, 1)
            split_x2(0)
            add_attention(b - 1, 1)
            denominator(b, 1)
            variance2(1)
            split_p(b, 0)
            normal_x2(2)
            gate_hidden(0, 0)
            split_hid(0, 0)
            add_attention(b, 0)
            split_p(b, 1)
            split_x2(2)
            gate_hidden(1, 1)
            split_hid(1, 1)
            add_attention(b, 1)
            variance2(2)
            normal_x2(3)
            split_x2(3)
            add_expert(0, 0)
            dve.wait_ge(lg_ps, 1)
            dve.tensor_copy(logits[:, :, :], bankS[:, 1, 0:NT * NE].rearrange("p (t e) -> p t e", e=NE)).then_inc(route, 1)
            dve.wait_ge(route, 1)
            dve.tensor_reduce(lmax[:, :], logits[:, :, :], AX.X, ALU.max).then_inc(route, 1)
            dve.wait_ge(route, 2)
            dve.tensor_tensor(logits[:, :, :], logits[:, :, :], lmax[:, :].unsqueeze(2).to_broadcast([P, NT, NE]),
                              ALU.subtract).then_inc(route, 1)
            split_w(JS, 0, JS % RS)
            split_w(JS + 1, 1, (JS + 1) % RS)
            gate_hidden(2, 2)
            gate_hidden(3, 3)
            split_hid(2, 2)
            dve.wait_ge(lexp_ok, 1)
            dve.tensor_reduce(lsum[:, :], lexp[:, :, :], AX.X, ALU.add).then_inc(route, 1)
            dve.wait_ge(route, 4)
            dve.reciprocal(lrcp[:, :], lsum[:, :]).then_inc(route, 1)
            dve.wait_ge(route, 5)
            dve.tensor_tensor(rp[:, :, :], lexp[:, :, :], lrcp[:, :].unsqueeze(2).to_broadcast([P, NT, NE]),
                              ALU.mult).then_inc(route, 1)
            dve.wait_ge(route, 6)
            pj = rp[:, :, :].unsqueeze(2).to_broadcast([P, NT, NE, NE])
            pe_ = rp[:, :, :].unsqueeze(3).to_broadcast([P, NT, NE, NE])

            def pairs(ap):
                return ap[:, :, :].rearrange("p t (e j) -> p t e j", e=NE)

            dve.tensor_tensor(pairs(gt), pj, pe_, ALU.is_gt).then_inc(route, 1)
            dve.tensor_tensor(pairs(eq), pj, pe_, ALU.is_equal).then_inc(route, 1)
            dve.wait_ge(route, 8)
            dve.tensor_tensor(eq[:, :, :], eq[:, :, :], before[:, :].unsqueeze(1).to_broadcast([P, NT, NE * NE]),
                              ALU.mult).then_inc(route, 1)
            dve.wait_ge(route, 9)
            dve.tensor_tensor(gt[:, :, :], gt[:, :, :], eq[:, :, :], ALU.add).then_inc(route, 1)
            dve.wait_ge(route, 10)
            dve.tensor_reduce(rank[:, :, :], pairs(gt), AX.X, ALU.add).then_inc(route, 1)
            dve.wait_ge(route, 11)
            dve.tensor_scalar(keep[:, :, :], rank[:, :, :], 2.0, tg[:, 1:2], ALU.is_lt, ALU.mult).then_inc(route, 1)
            dve.wait_ge(route, 12)
            dve.tensor_tensor(comb[:, NT:].rearrange("p (e t) -> p t e", t=NT), rp[:, :, :], keep[:, :, :], ALU.mult).then_inc(route, 1)
            dve.wait_ge(route, 13)

            def expert(e, first, last):
                base = e * 8 + 2 * JS
                for u in range(2 * JE):
                    gate_hidden(base + u, u)
                    split_hid(base + u - 1, u - 1 + 2 * JE)
                    if u < 2 and not (first and u == 0):
                        add_expert(e, u)
                    if u % 2 == 0 and not (last and u >= JE):
                        i = JS + u // 2 + 2
                        split_w(e * JE + i, (i + JS) % WS, i % RS)

            expert(0, True, False)
            with dve.Fori(1, NE - 1) as e:
                expert(e, False, False)
            expert(NE - 1, False, True)
            split_hid(2 * NM - 1, 2 * JE - 1)
            for c in range(NC):
                add_expert(NE, c, True)

        @block.gpsimd
        def _(pool):
            def split_wq(g, s):
                pool.wait_ge(wq_hi, g + 1)
                pool.tensor_tensor(w_lo[:, s, 0:2 * D], raw_kvq[:, s, 2 * HD:KVQ], w_hi[:, s, 0:2 * D].bitcast(F32),
                                   ALU.subtract).then_inc(wq_lo, 1)

            def normal_p(b, par):
                pool.wait_ge(rcp_ok, b * TPB + par + 1)
                pool.tensor_tensor(by_head(probs[:, par, :]), by_head(probs[:, par, :]),
                                   rcp[:, par, :].unsqueeze(2).to_broadcast([P, NH, S]), ALU.mult).then_inc(p_ok, 1)

            for s in range(2):
                split_wq(s, s)
            with pool.Fori(1, NG // 2) as it:
                for s in range(2):
                    split_wq(it * 2 + s, s)
            pool.wait_ge(mhalf_ok, 1)
            pool.wait_ge(vare_ok, 1)
            pool.tensor_tensor(rstd[:, :], vare[:, :], mhalf[:, :], ALU.pow).then_inc(rstd_ok, 1)
            normal_p(0, 0)
            normal_p(0, 1)
            with pool.Fori(1, NB - 1) as b:
                for par in range(TPB):
                    normal_p(b, par)
            for h, (t0, t1) in enumerate(PARTS):
                pool.wait_ge(vare2_ok, h + 1)
                pool.tensor_tensor(rstd2[:, t0:t1], vare2[:, t0:t1], mhalf[:, t0:t1], ALU.pow).then_inc(rstd2_ok, 1)
                if h == 0:
                    for par in range(TPB):
                        normal_p(NB - 1, par)
            pool.wait_ge(route, 3)
            pool.tensor_tensor(lexp[:, :, :], euler[:, :].rearrange("p (t e) -> p t e", e=NE), logits[:, :, :],
                               ALU.pow).then_inc(lexp_ok, 1)


def kernel(x, ctx_1024, mask_BxS2_bf1, g_xattn, g_ffn, L0_xattn_Wq, L0_xattn_Wk, L0_xattn_Wv, L0_xattn_Wo,
           L0_ffn_gate_w, L0_ffn_w1, L0_ffn_w3, L0_ffn_w2, L0_ffn_sw1, L0_ffn_sw3, L0_ffn_sw2):
    import numpy as np
    import concourse.bacc as bacc
    from concourse import mybir as _mybir
    from concourse.bass_utils import run_bass_kernel_spmd

    a = np.asarray
    kv = [a(w).reshape(DV, NG, HD).transpose(1, 0, 2) for w in (L0_xattn_Wk, L0_xattn_Wv)]
    wqT = a(L0_xattn_Wq).reshape(D, NG, 2, HD).transpose(1, 3, 2, 0).reshape(NG, HD, 2 * D)
    wo = a(L0_xattn_Wo).reshape(NG, 2, HD, D).transpose(0, 2, 1, 3).reshape(NG, HD, 2 * D)

    def hidden_tiles(w1, w3, w2):
        n = w1.shape[0] // P
        ups = [w.reshape(n, P, KD, P).transpose(0, 3, 2, 1).reshape(n, P, KD * P) for w in (w1, w3)]
        return np.concatenate(ups + [w2.T.reshape(n, P, D)], axis=2)

    tiles = [hidden_tiles(a(L0_ffn_sw1), a(L0_ffn_sw3), a(L0_ffn_sw2))]
    tiles += [hidden_tiles(a(L0_ffn_w1)[e], a(L0_ffn_w3)[e], a(L0_ffn_w2)[e]) for e in range(NE)]
    e, j = np.meshgrid(np.arange(NE), np.arange(NE), indexing="ij")
    arrays = {
        "x": a(x).reshape(NB * T, D),
        "ctxT": a(ctx_1024).transpose(2, 0, 1).reshape(DV, NB * S),
        "mask": np.broadcast_to(a(mask_BxS2_bf1).view(np.uint8).reshape(1, NB * S), (P, NB * S)),
        "gates": np.broadcast_to(np.concatenate([a(g_xattn), a(g_ffn)]).reshape(1, 2), (P, 2)),
        "kvq": np.concatenate(kv + [wqT], axis=2),
        "wo": wo,
        "gwT": a(L0_ffn_gate_w).reshape(NE, KD, P).transpose(2, 1, 0).reshape(P, KD * NE),
        "ffn": np.concatenate(tiles, axis=0),
        "ident": np.eye(P, dtype=np.float32),
        "before": np.broadcast_to((j < e).astype(np.float32).reshape(1, NE * NE), (P, NE * NE)),
    }
    nc = bacc.Bacc("TRN2", target_bir_lowering=False, num_devices=1)
    feed, args = {}, []
    for name, v in arrays.items():
        v = np.ascontiguousarray(v)
        feed[f"{name}_dram"] = v
        args.append(nc.dram_tensor(f"{name}_dram", v.shape, _mybir.dt.from_np(v.dtype), kind="ExternalInput").ap())
    out = nc.dram_tensor("out_dram", (NB * T, D), F32, kind="ExternalOutput").ap()
    build(nc, *args, out)
    r = run_bass_kernel_spmd(nc, [feed], core_ids=[0])
    return r.results[0]["out_dram"].reshape(NB, T, D)
```

```python
import math
from contextlib import ExitStack

import concourse.bass as bass
from concourse import mybir

F32 = mybir.dt.float32
F32R = mybir.dt.float32r
U8 = mybir.dt.uint8
ALU = mybir.AluOpType
ACT = mybir.ActivationFunctionType
AX = mybir.AxisListType

P = 128
NB, T, D = 4, 256, 256
S, DV = 64, 128
NH, NG, HD = 16, 8, 128
KD = D // P
NT = NB * T // P
TPB = T // P
NE, H, HS = 4, 512, 256
JE, JS = H // P, HS // P
NM = JS + NE * JE
WS = 4
RS = 2
HR = 4
CH = 512
TC = CH // P
NC = NB * T // CH
SW = NH * S
KVQ = 2 * HD + 2 * D
UPC = 2 * KD * P
FFC = UPC + D
SCALE = float(HD) ** -0.5
EPS = 1e-5
MASKED = 1e30
HALVES = [(0, 4), (4, 8)]
PARTS = [(0, 4), (4, 6), (6, 7), (7, 8)]
STORES = [(0, 2), (2, 4), (4, 6), (6, 7), (7, 8)]
TURN_AFTER = {2: 1, 3: 2}


def wait(eng, sem, n):
    if isinstance(n, int) and n <= 0:
        return
    eng.wait_ge(sem, n)


def build(nc, x, ctxT_kv0, mask, gates, kvq, wo, gwT, ffn, ident_c, before_c, out):
    with ExitStack() as ctx:
        def sb(name, shape, dt=F32):
            return ctx.enter_context(nc.sbuf_tensor(name, shape, dt))

        def sem(name):
            return ctx.enter_context(nc.semaphore(name))

        x_sb = sb("x_sb", [P, NT * D])
        A_hi = sb("A_hi", [P, KD, NB, SW], F32R)
        A_lo = sb("A_lo", [P, KD, NB, SW], F32R)
        VO_hi = sb("VO_hi", [P, NB, NG, D], F32R)
        VO_lo = sb("VO_lo", [P, NB, NG, D], F32R)
        xT_hi = sb("xT_hi", [P, KD, NT * P], F32R)
        xT_lo = sb("xT_lo", [P, KD, NT * P], F32R)
        PT_hi = sb("PT_hi", [P, NG, P], F32R)
        PT_lo = sb("PT_lo", [P, NG, P], F32R)
        w_hi = sb("w_hi", [P, WS, FFC], F32R)
        w_lo = sb("w_lo", [P, WS, FFC], F32R)
        raw = sb("raw", [P, RS, FFC])
        probs = sb("probs", [P, TPB, SW])
        xn0 = sb("xn0", [P, TPB, D])
        xn1 = sb("xn1", [P, TPB, D])
        ident = sb("ident", [P, P])
        before = sb("before", [P, NE * NE])
        mask_u8 = sb("mask_u8", [P, NB * S], U8)
        bias = sb("bias", [P, NB * S], F32R)
        onerow = sb("onerow", [P, P], F32R)
        anyvalid = sb("anyvalid", [P, NB])
        tga = sb("tga", [P, NB])
        gates_sb = sb("gates_sb", [P, 2])
        tg = sb("tg", [P, 2])
        gw_sb = sb("gw_sb", [P, KD * NE])
        gw = sb("gw", [P, KD, 2 * NE], F32R)
        stats = sb("stats", [P, NT * 6])
        mv = sb("mv", [P, NT * 2])
        stats2 = sb("stats2", [P, NT * 6])
        mv2 = sb("mv2", [P, NT * 2])
        vare = sb("vare", [P, NT])
        vare2 = sb("vare2", [P, NT])
        rstd = sb("rstd", [P, NT])
        mneg = sb("mneg", [P, NT])
        mrneg = sb("mrneg", [P, NT])
        rstd2 = sb("rstd2", [P, NT])
        mneg2 = sb("mneg2", [P, NT])
        mrneg2 = sb("mrneg2", [P, NT])
        mhalf = sb("mhalf", [P, NT])
        euler = sb("euler", [P, NT * NE])
        mx = sb("mx", [P, TPB, NH])
        den = sb("den", [P, TPB, NH])
        rcp = sb("rcp", [P, TPB, NH])
        logits = sb("logits", [P, NT, NE])
        lmax = sb("lmax", [P, NT])
        lexp = sb("lexp", [P, NT, NE])
        lsum = sb("lsum", [P, NT])
        lrcp = sb("lrcp", [P, NT])
        rp = sb("rp", [P, NT, NE])
        gt = sb("gt", [P, NT, NE * NE])
        eq = sb("eq", [P, NT, NE * NE])
        rank = sb("rank", [P, NT, NE])
        keep = sb("keep", [P, NT, NE])
        comb = sb("comb", [P, (1 + NE) * NT])

        raw_kvq = raw
        raw_wo = probs[:, 0, :].rearrange("p (s n) -> p s n", s=2)
        VT = probs[:, 1, 0:2 * NB * S].rearrange("p (s n) -> p s n", s=2)
        ctx_kv0 = probs[:, 1, 2 * NB * S:2 * NB * S + NB * S + 2 * HD]
        ctx_sb = ctx_kv0[:, 0:NB * S]
        KT_hi = PT_hi[:, 0:4, :].rearrange("p (s a) n -> p s (a n)", s=2)
        KT_lo = PT_lo[:, 0:4, :].rearrange("p (s a) n -> p s (a n)", s=2)
        mask_f = xn0[:, 0, :]
        first_tile = probs[:, 0, :].rearrange("p (a n) -> p a n", a=2)
        logitsT = probs[0:2 * NE, 1, :]
        xn = [xn1, xn0, xn0, xn1]
        hid_hi = A_hi[:, 0, 0:HR * CH // SW, :].rearrange("p a (b n) -> p (a b) n", n=CH)
        hid_lo = A_lo[:, 0, 0:HR * CH // SW, :].rearrange("p a (b n) -> p (a b) n", n=CH)
        hid_f = probs[:, 0, :].rearrange("p (s n) -> p s n", s=2)

        bankP, bankQ, bankR, bankS = [ctx.enter_context(nc.psum_tensor(f"bank{c}", [P, 2, 512], F32)) for c in "PQRS"]
        scores_ps = [bankP, bankQ]
        up_ps = [bankP, bankQ]
        acc_ps = [bankR, bankS]
        x2_bank = [bankR, bankS, bankS, bankS]

        ctx_ld, x_ld, const_ld = sem("ctx_ld"), sem("x_ld"), sem("const_ld")
        kvq_ld = [sem(f"kvq_ld{i}") for i in range(2)]
        wo_ld = [sem(f"wo_ld{i}") for i in range(2)]
        ffn_ld = [sem(f"ffn_ld{i}") for i in range(RS)]
        prep = sem("prep")
        onerow_ok, tg_ok = sem("onerow_ok"), sem("tg_ok")
        gwhi_ok, gwlo_ok = sem("gwhi_ok"), sem("gwlo_ok")
        kv_ps, k_hi, kv_sb = sem("kv_ps"), sem("k_hi"), sem("kv_sb")
        wq_hi, wq_lo = sem("wq_hi"), sem("wq_lo")
        a_ps, a_hi, a_lo = sem("a_ps"), sem("a_hi"), sem("a_lo")
        vo_ps, vo_hi, vo_lo = sem("vo_ps"), sem("vo_hi"), sem("vo_lo")
        st1, mv_ok, bias_ok, vare_ok, rstd_ok = sem("st1"), sem("mv_ok"), sem("bias_ok"), sem("vare_ok"), sem("rstd_ok")
        mrneg_ok, mhalf_ok = sem("mrneg_ok"), sem("mhalf_ok")
        xn_ok, xt_ps, xt_hi, xt_lo = sem("xn_ok"), sem("xt_ps"), sem("xt_hi"), sem("xt_lo")
        sc_half, mx_half, sub_half, exp_half = sem("sc_half"), sem("mx_half"), sem("sub_half"), sem("exp_half")
        sc_ps, mx_ok, sub_ok, exp_ok = sem("sc_ps"), sem("mx_ok"), sem("sub_ok"), sem("exp_ok")
        den_ok, rcp_ok, p_ok = sem("den_ok"), sem("rcp_ok"), sem("p_ok")
        pt_ps, pt_hi, pt_lo = sem("pt_ps"), sem("pt_hi"), sem("pt_lo")
        pv_ps, x1_ok, st2, mv2_ok = sem("pv_ps"), sem("x1_ok"), sem("st2"), sem("mv2_ok")
        vare2_ok, rstd2_ok, mrneg2_ok = sem("vare2_ok"), sem("rstd2_ok"), sem("mrneg2_ok")
        xn2_ok, x2_ps, x2_hi, x2_lo = ([sem(f"{n}{c}") for c in range(NT // TPB)] for n in ("xn2_ok", "x2_ps", "x2_hi", "x2_lo"))
        lgT_ps, lgT_sb = sem("lgT_ps"), sem("lgT_sb")
        lg_ps, route, lexp_ok = sem("lg_ps"), sem("route"), sem("lexp_ok")
        wf_hi, wf_lo = sem("wf_hi"), sem("wf_lo")
        u_ps, g_ps, silu_ok, hid_ok = sem("u_ps"), sem("g_ps"), sem("silu_ok"), sem("hid_ok")
        hid_hi_ok, hid_lo_ok = sem("hid_hi_ok"), sem("hid_lo_ok")
        down_ps, final_ps, y_ok, out_ok, stored = sem("down_ps"), sem("final_ps"), sem("y_ok"), sem("out_ok"), sem("stored")

        def split3(eng, acc, l_hi, l_lo, r_hi, r_lo, start, stop, **kw):
            eng.matmul(acc, l_hi, r_hi, start=start, stop=False, **kw)
            eng.matmul(acc, l_hi, r_lo, start=False, stop=False, **kw)
            return eng.matmul(acc, l_lo, r_hi, start=False, stop=stop, **kw)

        def by_head(ap):
            return ap.rearrange("p (h s) -> p h s", s=S)

        def normal_p(eng, par):
            eng.tensor_tensor(by_head(probs[:, par, :]), by_head(probs[:, par, :]),
                              rcp[:, par, :].unsqueeze(2).to_broadcast([P, NH, S]), ALU.mult).then_inc(p_ok, 1)

        def split_w(eng, m, s, r):
            eng.wait_ge(wf_hi, m + 1)
            eng.tensor_tensor(w_lo[:, s, :], raw[:, r, :], w_hi[:, s, :].bitcast(F32), ALU.subtract).then_inc(wf_lo, 1)

        def at(b):
            return TPB if isinstance(b, int) and b == 0 else 0

        def xtile(n):
            return x_sb[:, bass.ds(n * D, D)]

        block = ctx.enter_context(nc.Block())

        @block.sync
        def _(sp):
            def load_kvq(g, s):
                sp.wait_ge(kv_ps, g - 1)
                sp.wait_ge(wq_lo, g - 1)
                sp.dma_start(raw_kvq[:, s, :], kvq[bass.ds(g, 1), :, :].rearrange("g p n -> p (g n)")).then_inc(kvq_ld[s], 16)

            def load_wo(g, s):
                sp.wait_ge(vo_ps, (g - 1) * 2)
                sp.dma_start(raw_wo[:, s, :], wo[bass.ds(g, 1), :, :].rearrange("g p n -> p (g n)")).then_inc(wo_ld[s], 16)

            def load_ffn(m, s):
                wait(sp, wf_lo, m - RS + 1)
                sp.dma_start(raw[:, s, :], ffn[bass.ds(m, 1), :, :].rearrange("g p n -> p (g n)")).then_inc(ffn_ld[s], 16)

            sp.dma_start(ctx_kv0[:, :], ctxT_kv0).then_inc(ctx_ld, 16)
            sp.dma_start(raw_kvq[:, 0, 2 * HD:], kvq[0, :, 2 * HD:]).then_inc(kvq_ld[0], 16)
            sp.dma_start(raw_kvq[:, 1, :], kvq[1]).then_inc(kvq_ld[1], 16)
            sp.dma_start(raw_wo[:, 0, :], wo[0]).then_inc(wo_ld[0], 16)
            sp.dma_start(raw_wo[:, 1, :], wo[1]).then_inc(wo_ld[1], 16)
            sp.dma_start(mask_u8[:, :], mask).then_inc(const_ld, 16)
            sp.dma_start(gates_sb[:, :], gates).then_inc(const_ld, 16)
            sp.dma_start(ident[:, :], ident_c).then_inc(const_ld, 16)
            sp.dma_start(before[:, :], before_c).then_inc(const_ld, 16)
            sp.dma_start(gw_sb[:, :], gwT).then_inc(const_ld, 16)
            load_kvq(2, 0)
            sp.dma_start(x_sb[:, :].rearrange("p (t d) -> p t d", d=D), x.rearrange("(t p) d -> p t d", p=P)).then_inc(x_ld, 16)
            load_wo(2, 0)
            load_kvq(3, 1)
            load_wo(3, 1)
            with sp.Fori(2, NG // 2) as it:
                for s in range(2):
                    load_kvq(it * 2 + s, s)
                    load_wo(it * 2 + s, s)
            sp.wait_ge(wq_lo, NG)
            sp.wait_ge(vo_ps, 2 * NG)
            for s in range(RS):
                load_ffn(s, s)
            with sp.Fori(1, NM // RS) as it:
                for s in range(RS):
                    load_ffn(it * RS + s, s)
            for t0, t1 in STORES:
                sp.wait_ge(out_ok, t1)
                sp.dma_start(out.rearrange("(t p) d -> p t d", p=P)[:, t0:t1, :],
                             x_sb[:, t0 * D:t1 * D].rearrange("p (t d) -> p t d", d=D)).then_inc(stored, 16)
            sp.wait_ge(stored, 16 * len(STORES))

        @block.tensor
        def _(pe):
            def keys_values(g, s, n):
                if isinstance(g, int) and g == 0:
                    pe.wait_ge(ctx_ld, 16)
                    w = ctx_kv0[:, NB * S:]
                else:
                    pe.wait_ge(kvq_ld[s], (n + 1) * 16)
                    w = raw_kvq[:, s, 0:2 * HD]
                wait(pe, kv_sb, g - 1)
                pe.matmul(bankP[:, s, 0:NB * S], w[:, 0:HD], ctx_sb[:, :], start=True, stop=True)
                pe.matmul(bankP[:, s, NB * S:], w[:, HD:], ctx_sb[:, :], start=True, stop=True).then_inc(kv_ps, 1)

            def query_side(g, s):
                pe.wait_ge(kv_sb, g + 1)
                pe.wait_ge(wq_lo, g + 1)
                for hh in range(2):
                    wait(pe, a_lo, (g - 1) * 2 + hh + 1)
                    for k in range(KD):
                        c = hh * D + k * P
                        mm = split3(pe, bankQ[:, hh, k * D:(k + 1) * D], w_hi[:, s, c:c + P], w_lo[:, s, c:c + P],
                                    KT_hi[:, s, :], KT_lo[:, s, :], True, True)
                    mm.then_inc(a_ps, 1)

            def output_side(g, s, n):
                pe.wait_ge(wo_ld[s], (n + 1) * 16)
                for pair in range(2):
                    wait(pe, vo_lo, (g - 1) * 2 + pair + 1)
                    for r in range(2):
                        b = pair * 2 + r
                        for hh in range(2):
                            mm = pe.matmul(bankR[hh * S:(hh + 1) * S, pair, r * D:(r + 1) * D], VT[:, s, b * S:(b + 1) * S],
                                           raw_wo[:, s, hh * D:(hh + 1) * D], start=True, stop=True)
                    mm.then_inc(vo_ps, 1)

            def heads(it):
                g = it * 2
                keys_values(g + 1, 1, it)
                query_side(g, 0)
                output_side(g, 0, it)
                keys_values(g + 2, 0, it + 1)
                query_side(g + 1, 1)
                output_side(g + 1, 1, it)

            def turn_x(b):
                pe.wait_ge(xn_ok, (b + 1) * TPB)
                wait(pe, xt_lo, b)
                for par in range(TPB):
                    for k in range(KD):
                        c = (par * KD + k) * P
                        mm = pe.transpose(bankS[:, 0, c:c + P], xn0[:, par, k * P:(k + 1) * P], ident[:, :])
                mm.then_inc(xt_ps, 1)

            def scores_half(b, par, hf):
                t = slice((at(b) + par) * P, (at(b) + par + 1) * P)
                acc = scores_ps[par][:, hf, :]
                pe.matmul(acc, onerow[:, :], bias[:, bass.ds(b * S, S)].unsqueeze(1).to_broadcast([P, NH // 2, S]),
                          start=True, stop=False)
                for k in range(KD):
                    mm = split3(pe, acc, xT_hi[:, k, t], xT_lo[:, k, t],
                                A_hi[:, k, bass.ds(b, 1), hf * 512:(hf + 1) * 512].rearrange("p a n -> p (a n)"),
                                A_lo[:, k, bass.ds(b, 1), hf * 512:(hf + 1) * 512].rearrange("p a n -> p (a n)"),
                                False, k == KD - 1)
                return mm

            def scores_wait(b, par):
                pe.wait_ge(xt_lo, b + 1)
                wait(pe, sub_ok, b * TPB + par - 1)

            def scores(b, par):
                scores_wait(b, par)
                scores_half(b, par, 0)
                scores_half(b, par, 1).then_inc(sc_ps, 1)

            def turn_p(b, par):
                n = b * TPB + par
                pe.wait_ge(p_ok, n + 1)
                for q in range(2):
                    for g in range(NG // 2):
                        c = (q * NG // 2 + g) * P
                        mm = pe.transpose(bankR[:, q, g * P:(g + 1) * P], probs[:, par, c:c + P], ident[:, :])
                    mm.then_inc(pt_ps, 1)

            def attend_half(b, par, q):
                pe.wait_ge(pt_lo, (b * TPB + par) * 2 + q + 1)
                for g in range(q * NG // 2, (q + 1) * NG // 2):
                    mm = split3(pe, bankS[:, 1, 0:D], PT_hi[:, g, :], PT_lo[:, g, :],
                                VO_hi[:, bass.ds(b, 1), g, :].rearrange("p a n -> p (a n)"),
                                VO_lo[:, bass.ds(b, 1), g, :].rearrange("p a n -> p (a n)"), g == 0, g == NG - 1)
                return mm

            def attend(b, par):
                attend_half(b, par, 0)
                attend_half(b, par, 1).then_inc(pv_ps, 1)

            def attend_batch(b):
                scores(b, 1)
                turn_x(b + 1)
                attend(b - 1, 0)
                turn_p(b - 1, 1)
                scores(b + 1, 0)
                attend(b - 1, 1)
                turn_p(b, 0)

            def turn_x2(c):
                pe.wait_ge(xn2_ok[c], TPB)
                if c in TURN_AFTER:
                    pe.wait_ge(x2_lo[TURN_AFTER[c]], 1)
                for par in range(TPB):
                    for k in range(KD):
                        o = (par * KD + k) * P
                        mm = pe.transpose(x2_bank[c][:, 0, o:o + P], xn[c][:, par, k * P:(k + 1) * P], ident[:, :])
                mm.then_inc(x2_ps[c], 1)

            def route_chunk(c):
                acc = bankS[0:2 * NE, 1 - c, :]
                for k in range(KD):
                    for i, half in enumerate((xT_hi, xT_lo)):
                        mm = pe.matmul(acc, gw[:, k, :], half[:, k, c * CH:(c + 1) * CH], start=k + i == 0, stop=k + i == KD)
                mm.then_inc(lgT_ps, 1)

            def turn_logits():
                for t in range(NT):
                    mm = pe.transpose(bankS[:, 1, t * 2 * NE:(t + 1) * 2 * NE], logitsT[:, t * P:(t + 1) * P], ident[0:2 * NE, 0:2 * NE])
                mm.then_inc(lg_ps, 1)

            def up_unit(u, s, c):
                for mat, done in ((0, u_ps), (1, g_ps)):
                    for k in range(KD):
                        o = (mat * KD + k) * P
                        mm = split3(pe, up_ps[u % 2][:, mat, :], w_hi[:, s, o:o + P], w_lo[:, s, o:o + P],
                                    xT_hi[:, k, c * CH:(c + 1) * CH], xT_lo[:, k, c * CH:(c + 1) * CH], k == 0, k == KD - 1)
                    mm.then_inc(done, 1)

            def down_unit(n, u, s, c, first, last, e, final=False):
                pe.wait_ge(hid_lo_ok, n + 1)
                if first:
                    wait(pe, y_ok, (e - 1) * NC + c + 1)
                for tt in range(TC):
                    o = tt * P
                    mm = split3(pe, acc_ps[c][:, tt // 2, tt % 2 * D:(tt % 2 + 1) * D],
                                hid_hi[:, u % HR, o:o + P], hid_lo[:, u % HR, o:o + P],
                                w_hi[:, s, UPC:FFC], w_lo[:, s, UPC:FFC],
                                first and tt % 2 == 0, last, skip_group_check=True)
                    if final and tt % 2 == 1:
                        mm.then_inc(final_ps, 1)
                if not final:
                    mm.then_inc(down_ps, 1)

            keys_values(0, 0, 0)
            heads(0)
            with pe.Fori(1, NG // 2 - 1) as it:
                heads(it)
            pe.wait_ge(const_ld, 80)
            it = NG // 2 - 1
            keys_values(NG - 1, 1, it)
            query_side(NG - 2, 0)
            output_side(NG - 2, 0, it)
            query_side(NG - 1, 1)
            turn_x(0)
            output_side(NG - 1, 1, it)
            pe.wait_ge(onerow_ok, 1)
            pe.wait_ge(bias_ok, 1)
            pe.wait_ge(kv_sb, NG)
            pe.wait_ge(a_lo, 2 * NG)
            scores_wait(0, 0)
            scores_half(0, 0, 0).then_inc(sc_half, 1)
            scores_half(0, 0, 1).then_inc(sc_ps, 1)
            turn_x(1)
            scores(0, 1)
            scores(1, 0)
            pe.wait_ge(vo_lo, 2 * NG)
            turn_p(0, 0)
            with pe.Fori(1, NB - 1) as b:
                attend_batch(b)
            b = NB - 1
            scores_wait(b, 1)
            scores_half(b, 1, 0)
            attend(b - 1, 0)
            turn_p(b - 1, 1)
            scores_half(b, 1, 1).then_inc(sc_ps, 1)
            turn_x2(1)
            attend_half(b - 1, 1, 0)
            pe.wait_ge(pt_lo, 2 * (NT - TPB))
            turn_x2(0)
            attend_half(b - 1, 1, 1).then_inc(pv_ps, 1)
            pe.wait_ge(x2_lo[0], 1)
            turn_p(b, 0)
            pe.wait_ge(wf_lo, 1)
            pe.wait_ge(sub_ok, NT - 1)
            pe.wait_ge(x2_lo[0], 1)
            up_unit(0, JS, 0)
            attend(b, 0)
            turn_p(b, 1)
            pe.wait_ge(wf_lo, 2)
            pe.wait_ge(sub_ok, NT)
            up_unit(1, JS + 1, 0)
            turn_x2(2)
            attend(b, 1)
            down_unit(0, 0, JS, 0, True, False, 0)
            pe.wait_ge(gwlo_ok, 1)
            pe.wait_ge(x1_ok, NT)
            route_chunk(0)
            turn_x2(3)
            down_unit(1, 1, JS + 1, 0, False, True, 0)
            pe.wait_ge(x2_lo[2], 1)
            pe.wait_ge(x2_lo[3], 1)
            route_chunk(1)
            pe.wait_ge(hid_ok, 1)
            up_unit(2, JS, 1)
            pe.wait_ge(lgT_sb, NC)
            turn_logits()
            pe.wait_ge(hid_ok, 2)
            up_unit(3, JS + 1, 1)
            pe.wait_ge(route, 1)

            def expert(e, first):
                base = e * JE * NC + JS * NC
                for u in range(2 * JE):
                    n = base + u
                    pe.wait_ge(wf_lo, e * JE + JS + u // 2 + 1)
                    pe.wait_ge(hid_ok, n - 1)
                    up_unit(u, u // 2, u % 2)
                    if u >= 2:
                        down_unit(n - 2, u - 2, u // 2 - 1, u % 2, u < 4, False, e + 1)
                    elif first:
                        down_unit(n - 2, u + 2, JS + u, 1, u == 0, u == 1, 0)
                    else:
                        down_unit(n - 2, u + 2 * JE - 2, WS - 1, u, False, True, e)

            expert(0, True)
            with pe.Fori(1, NE) as e:
                expert(e, False)
            for u in range(2):
                n = 2 * NM - 2 + u
                down_unit(n, u + 2 * JE - 2, WS - 1, u, False, True, NE, True)

        @block.scalar
        def _(act):
            def split_wq(g, s, n):
                act.wait_ge(kvq_ld[s], (n + 1) * 16)
                wait(act, a_ps, (g - 1) * 2)
                act.copy(w_hi[:, s, 0:2 * D], raw_kvq[:, s, 2 * HD:KVQ]).then_inc(wq_hi, 1)

            def split_k(g, s):
                act.wait_ge(kv_ps, g + 1)
                act.copy(KT_hi[:, s, :], bankP[:, s, 0:NB * S]).then_inc(k_hi, 1)

            def evict_query_side(g):
                for hh in range(2):
                    act.wait_ge(a_ps, g * 2 + hh + 1)
                    act.copy(A_hi[:, :, :, bass.ds(g * 2 * S + hh * S, S)],
                             bankQ[:, hh, :].rearrange("p (k b s) -> p k b s", k=KD, b=NB)).then_inc(a_hi, 1)

            def evict_output_side(g):
                for pair in range(2):
                    act.wait_ge(vo_ps, g * 2 + pair + 1)
                    act.copy(VO_hi[:, pair * 2:pair * 2 + 2, bass.ds(g, 1), :].rearrange("p b a n -> p b (a n)"),
                             bankR[:, pair, :].rearrange("p (b n) -> p b n", b=2)).then_inc(vo_hi, 1)

            def heads(it):
                g = it * 2
                split_wq(g + 1, 1, it)
                split_k(g + 1, 1)
                evict_query_side(g)
                evict_output_side(g)
                split_wq(g + 2, 0, it + 1)
                split_k(g + 2, 0)
                evict_query_side(g + 1)
                evict_output_side(g + 1)

            def split_x(b):
                act.wait_ge(xt_ps, b + 1)
                if not isinstance(b, int):
                    act.wait_ge(sc_ps, b * TPB)
                act.copy(xT_hi[:, :, at(b) * P:(at(b) + TPB) * P].rearrange("p k (t n) -> p t k n", n=P),
                         bankS[:, 0, :].rearrange("p (t k n) -> p t k n", t=TPB, k=KD)).then_inc(xt_hi, 1)

            def exponent(b, par):
                act.wait_ge(sub_ok, b * TPB + par + 1)
                act.activation(probs[:, par, :], probs[:, par, :], ACT.Exp, scale=SCALE).then_inc(exp_ok, 1)

            def split_p(b, par):
                n = b * TPB + par
                for q in range(2):
                    act.wait_ge(pt_ps, n * 2 + q + 1)
                    act.copy(PT_hi[:, q * NG // 2:(q + 1) * NG // 2, :],
                             bankR[:, q, :].rearrange("p (g n) -> p g n", n=P)).then_inc(pt_hi, 1)

            def normal_x(b):
                wait(act, xt_ps, b)
                for par in range(TPB):
                    n = b * TPB + par
                    act.activation(xn0[:, par, :], xtile(n), ACT.Identity, bias=mrneg[:, bass.ds(n, 1)],
                                   scale=rstd[:, bass.ds(n, 1)]).then_inc(xn_ok, 1)

            def attend_batch(b):
                split_p(b - 1, 0)
                normal_x(b + 1)
                split_x(b + 1)
                exponent(b, 0)
                split_p(b - 1, 1)
                exponent(b, 1)

            def normal_x2(c):
                act.wait_ge(mrneg2_ok, 1)
                for n in range(c * TPB, (c + 1) * TPB):
                    act.activation(xn[c][:, n % TPB, :], xtile(n), ACT.Identity, bias=mrneg2[:, n:n + 1],
                                   scale=rstd2[:, n:n + 1]).then_inc(xn2_ok[c], 1)

            def split_x2(c):
                act.wait_ge(x2_ps[c], 1)
                act.copy(xT_hi[:, :, c * TPB * P:(c + 1) * TPB * P].rearrange("p k (t n) -> p t k n", n=P),
                         x2_bank[c][:, 0, :].rearrange("p (t k n) -> p t k n", t=TPB, k=KD)).then_inc(x2_hi[c], 1)

            def split_w(m, s, r, n):
                act.wait_ge(ffn_ld[r], (n + 1) * 16)
                wait(act, down_ps, 3 if isinstance(m, int) and m == WS else (m - WS) * 2 + 2)
                act.copy(w_hi[:, s, :], raw[:, r, :]).then_inc(wf_hi, 1)

            def silu(n, u):
                act.wait_ge(u_ps, n + 1)
                wait(act, hid_lo_ok, n - 1)
                act.activation(hid_f[:, u % 2, :], up_ps[u % 2][:, 0, :], ACT.Silu).then_inc(silu_ok, 1)

            def split_hid(n, u):
                act.wait_ge(hid_ok, n + 1)
                wait(act, down_ps, n - HR + 1)
                act.copy(hid_hi[:, u % HR, :], hid_f[:, u % 2, :]).then_inc(hid_hi_ok, 1)

            split_wq(0, 0, 0)
            split_k(0, 0)
            heads(0)
            act.wait_ge(const_ld, 80)
            act.activation(tg[:, :], gates_sb[:, :], ACT.Tanh).then_inc(tg_ok, 1)
            act.copy(gw[:, :, 0:NE], gw_sb[:, :].rearrange("p (k e) -> p k e", k=KD)).then_inc(gwhi_ok, 1)
            with act.Fori(1, NG // 2 - 1) as it:
                heads(it)
            act.wait_ge(mrneg_ok, 1)
            normal_x(0)
            split_wq(NG - 1, 1, NG // 2 - 1)
            split_k(NG - 1, 1)
            evict_query_side(NG - 2)
            evict_output_side(NG - 2)
            evict_query_side(NG - 1)
            split_x(0)
            evict_output_side(NG - 1)
            normal_x(1)
            split_w(0, JS, 0, 0)
            for hf, ready, done in ((0, sub_half, exp_half), (1, sub_ok, exp_ok)):
                act.wait_ge(ready, 1)
                act.activation(first_tile[:, hf, :], first_tile[:, hf, :], ACT.Exp, scale=SCALE).then_inc(done, 1)
                if hf == 0:
                    split_x(1)
            split_w(1, JS + 1, 1, 0)
            exponent(0, 1)
            act.wait_ge(mrneg_ok, 2)
            with act.Fori(1, NB - 1) as b:
                attend_batch(b)
            b = NB - 1
            split_p(b - 1, 0)
            exponent(b, 0)
            normal_x2(1)
            split_p(b - 1, 1)
            normal_x2(0)
            split_x2(1)
            split_x2(0)
            split_p(b, 0)
            exponent(b, 1)
            silu(0, 0)
            split_hid(0, 0)
            split_p(b, 1)
            silu(1, 1)
            split_x2(2)
            split_hid(1, 1)
            act.wait_ge(lgT_ps, 1)
            act.copy(logitsT[:, 0:CH], bankS[0:2 * NE, 1, :]).then_inc(lgT_sb, 1)
            split_x2(3)
            act.wait_ge(lgT_ps, 2)
            act.copy(logitsT[:, CH:], bankS[0:2 * NE, 0, :]).then_inc(lgT_sb, 1)
            for m in (JS, JS + 1):
                split_w(m, m - JS, m % RS, m // RS)
            silu(2, 2)
            silu(3, 3)
            split_hid(2, 2)

            def expert(e, last):
                base = e * JE * NC + JS * NC
                for u in range(2 * JE):
                    silu(base + u, u)
                    split_hid(base + u - 1, u - 1 + 2 * JE)
                    if u % 2 == 0 and not (last and u >= JE):
                        i = JS + u // 2 + 2
                        split_w(e * JE + i, (i + JS) % WS, i % RS, e * (JE // RS) + i // RS)

            expert(0, False)
            with act.Fori(1, NE - 1) as e:
                expert(e, False)
            expert(NE - 1, True)
            split_hid(2 * NM - 1, 2 * JE - 1)

        @block.vector
        def _(dve):
            def split_kv(g, s):
                dve.wait_ge(k_hi, g + 1)
                dve.tensor_tensor(KT_lo[:, s, :], bankP[:, s, 0:NB * S], KT_hi[:, s, :].bitcast(F32), ALU.subtract)
                wait(dve, vo_ps, (g - 1) * 2)
                dve.tensor_copy(VT[:, s, :], bankP[:, s, NB * S:]).then_inc(kv_sb, 1)

            def evict_query_side(g):
                for hh in range(2):
                    dve.wait_ge(a_hi, g * 2 + hh + 1)
                    o = bass.ds(g * 2 * S + hh * S, S)
                    dve.tensor_tensor(A_lo[:, :, :, o], bankQ[:, hh, :].rearrange("p (k b s) -> p k b s", k=KD, b=NB),
                                      A_hi[:, :, :, o].bitcast(F32), ALU.subtract).then_inc(a_lo, 1)

            def evict_output_side(g):
                for pair in range(2):
                    dve.wait_ge(vo_hi, g * 2 + pair + 1)
                    dve.tensor_tensor(VO_lo[:, pair * 2:pair * 2 + 2, bass.ds(g, 1), :].rearrange("p b a n -> p b (a n)"),
                                      bankR[:, pair, :].rearrange("p (b n) -> p b n", b=2),
                                      VO_hi[:, pair * 2:pair * 2 + 2, bass.ds(g, 1), :].rearrange("p b a n -> p b (a n)").bitcast(F32),
                                      ALU.subtract).then_inc(vo_lo, 1)

            def heads(it, between=lambda: None):
                g = it * 2
                split_kv(g + 1, 1)
                evict_query_side(g)
                evict_output_side(g)
                between()
                split_kv(g + 2, 0)
                evict_query_side(g + 1)
                evict_output_side(g + 1)

            def mask_row():
                dve.wait_ge(const_ld, 80)
                dve.tensor_copy(mask_f[:, :], mask_u8[:, :]).then_inc(prep, 1)
                dve.wait_ge(prep, 2)
                dve.tensor_scalar(bias[:, :], mask_f[:, :], -1.0, MASKED, ALU.add, ALU.mult).then_inc(bias_ok, 1)
                dve.tensor_reduce(anyvalid[:, :], mask_f[:, :].rearrange("p (b s) -> p b s", s=S), AX.X, ALU.max).then_inc(prep, 1)

            def split_x(b):
                dve.wait_ge(xt_hi, b + 1)
                for par in range(TPB):
                    o = slice((at(b) + par) * P, (at(b) + par + 1) * P)
                    ins = dve.tensor_tensor(xT_lo[:, :, o], bankS[:, 0, par * D:(par + 1) * D].rearrange("p (k n) -> p k n", k=KD),
                                            xT_hi[:, :, o].bitcast(F32), ALU.subtract)
                ins.then_inc(xt_lo, 1)

            def by_head_ps(par):
                return scores_ps[par][:, :, :].rearrange("p a (h s) -> p (a h) s", s=S)

            def maximum(b, par):
                dve.wait_ge(sc_ps, b * TPB + par + 1)
                dve.tensor_reduce(mx[:, par, :], by_head_ps(par), AX.X, ALU.max).then_inc(mx_ok, 1)

            def less_max(b, par):
                dve.wait_ge(mx_ok, b * TPB + par + 1)
                dve.tensor_tensor(by_head(probs[:, par, :]), by_head_ps(par), mx[:, par, :].unsqueeze(2).to_broadcast([P, NH, S]),
                                  ALU.subtract).then_inc(sub_ok, 1)

            def denominator(b, par):
                dve.wait_ge(exp_ok, b * TPB + par + 1)
                dve.tensor_reduce(den[:, par, :], by_head(probs[:, par, :]), AX.X, ALU.add).then_inc(den_ok, 1)

            def reciprocal(b, par):
                dve.wait_ge(den_ok, b * TPB + par + 1)
                dve.reciprocal(rcp[:, par, :], den[:, par, :]).then_inc(rcp_ok, 1)

            def finish_x(h):
                t0, t1 = HALVES[h]
                dve.wait_ge(st1, t1)
                for n in range(t0, t1):
                    dve.bn_aggr(mv[:, n * 2:n * 2 + 2], stats[:, n * 6:n * 6 + 6]).then_inc(mv_ok, 1)
                dve.wait_ge(mv_ok, t1)
                by_tile = mv[:, :].rearrange("p (t c) -> p t c", c=2)[:, t0:t1, :]
                dve.tensor_scalar(mneg[:, t0:t1], by_tile[:, :, 0], -1.0, None, ALU.mult)
                dve.tensor_scalar(vare[:, t0:t1], by_tile[:, :, 1], EPS, None, ALU.add).then_inc(vare_ok, 1)

            def split_p(b, par):
                n = b * TPB + par
                for q in range(2):
                    dve.wait_ge(pt_hi, n * 2 + q + 1)
                    o = slice(q * NG // 2, (q + 1) * NG // 2)
                    dve.tensor_tensor(PT_lo[:, o, :], bankR[:, q, :].rearrange("p (g n) -> p g n", n=P),
                                      PT_hi[:, o, :].bitcast(F32), ALU.subtract).then_inc(pt_lo, 1)

            def add_attention(b, par):
                n = b * TPB + par
                dve.wait_ge(pv_ps, n + 1)
                dve.scalar_tensor_tensor(xtile(n), bankS[:, 1, 0:D], tga[:, bass.ds(b, 1)], xtile(n), ALU.mult, ALU.add).then_inc(x1_ok, 1)

            def statistics(b, par):
                n = b * TPB + par
                dve.wait_ge(x1_ok, n + 1)
                dve.bn_stats(stats2[:, bass.ds(n * 6, 6)], xtile(n)).then_inc(st2, 1)

            def attend_batch(b):
                split_p(b - 1, 0)
                less_max(b, 0)
                maximum(b, 1)
                split_x(b + 1)
                denominator(b, 0)
                add_attention(b - 1, 0)
                reciprocal(b, 0)
                statistics(b - 1, 0)
                split_p(b - 1, 1)
                less_max(b, 1)
                maximum(b + 1, 0)
                denominator(b, 1)
                add_attention(b - 1, 1)
                reciprocal(b, 1)
                statistics(b - 1, 1)

            def variance2(h):
                t0, t1 = PARTS[h]
                dve.wait_ge(st2, t1)
                for n in range(t0, t1):
                    dve.bn_aggr(mv2[:, n * 2:n * 2 + 2], stats2[:, n * 6:n * 6 + 6]).then_inc(mv2_ok, 1)
                dve.wait_ge(mv2_ok, t1)
                by_tile = mv2[:, :].rearrange("p (t c) -> p t c", c=2)[:, t0:t1, :]
                if h == 0:
                    dve.tensor_scalar(mneg2[:, t0:t1], by_tile[:, :, 0], -1.0, None, ALU.mult)
                dve.tensor_scalar(vare2[:, t0:t1], by_tile[:, :, 1], EPS, None, ALU.add).then_inc(vare2_ok, 1)

            def normal_x2(h):
                dve.wait_ge(rstd2_ok, h + 1)
                for n in range(*PARTS[h]):
                    c = n // TPB
                    if n % TPB == 0 and c in TURN_AFTER:
                        dve.wait_ge(x2_ps[TURN_AFTER[c]], 1)
                    dve.tensor_scalar(xn[c][:, n % TPB, :], xtile(n), mv2[:, n * 2:n * 2 + 1], rstd2[:, n:n + 1],
                                      ALU.subtract, ALU.mult).then_inc(xn2_ok[c], 1)

            def split_x2(c):
                dve.wait_ge(x2_hi[c], 1)
                o = slice(c * TPB * P, (c + 1) * TPB * P)
                dve.tensor_tensor(xT_lo[:, :, o].rearrange("p k (t n) -> p t k n", n=P),
                                  x2_bank[c][:, 0, :].rearrange("p (t k n) -> p t k n", t=TPB, k=KD),
                                  xT_hi[:, :, o].rearrange("p k (t n) -> p t k n", n=P).bitcast(F32),
                                  ALU.subtract).then_inc(x2_lo[c], 1)

            def gate_hidden(n, u):
                dve.wait_ge(silu_ok, n + 1)
                dve.wait_ge(g_ps, n + 1)
                dve.tensor_tensor(hid_f[:, u % 2, :], up_ps[u % 2][:, 1, :], hid_f[:, u % 2, :], ALU.mult).then_inc(hid_ok, 1)

            def split_hid(n, u):
                dve.wait_ge(hid_hi_ok, n + 1)
                dve.tensor_tensor(hid_lo[:, u % HR, :], hid_f[:, u % 2, :], hid_hi[:, u % HR, :].bitcast(F32),
                                  ALU.subtract).then_inc(hid_lo_ok, 1)

            def add_expert(e, c, final=False):
                if not final:
                    dve.wait_ge(down_ps, JS if isinstance(e, int) and e == 0 and c == 0 else e * JE * NC + JS * NC - 1 + c)
                for tt in range(TC):
                    t = c * TC + tt
                    if final and tt % 2 == 0:
                        dve.wait_ge(final_ps, t // 2 + 1)
                    ins = dve.scalar_tensor_tensor(x_sb[:, t * D:(t + 1) * D], acc_ps[c][:, tt // 2, tt % 2 * D:(tt % 2 + 1) * D],
                                                   comb[:, bass.ds(e * NT + t, 1)], x_sb[:, t * D:(t + 1) * D], ALU.mult, ALU.add)
                    if final:
                        ins.then_inc(out_ok, 1)
                if not final:
                    ins.then_inc(y_ok, 1)

            dve.memset(onerow[:, :].bitcast(F32), 0.0).then_inc(prep, 1)
            dve.wait_ge(prep, 1)
            dve.memset(onerow[0:1, :].bitcast(F32), 1.0).then_inc(onerow_ok, 1)
            dve.memset(mhalf[:, :], -0.5)
            dve.memset(euler[:, :], math.e).then_inc(mhalf_ok, 1)
            split_kv(0, 0)
            heads(0, mask_row)
            dve.wait_ge(x_ld, 16)
            for n in range(NT // 2):
                dve.bn_stats(stats[:, n * 6:n * 6 + 6], xtile(n)).then_inc(st1, 1)
            finish_x(0)
            with dve.Fori(1, NG // 2 - 1) as it:
                heads(it)
                for i in range(NT // 4):
                    n = it * (NT // 4) + i + NT // 4
                    dve.bn_stats(stats[:, bass.ds(n * 6, 6)], xtile(n)).then_inc(st1, 1)
            split_kv(NG - 1, 1)
            evict_query_side(NG - 2)
            evict_output_side(NG - 2)
            evict_query_side(NG - 1)
            split_x(0)
            evict_output_side(NG - 1)
            finish_x(1)
            by_half = (slice(0, NH // 2), slice(NH // 2, NH))
            for hf, ready, mx_done, sub_done in ((0, sc_half, mx_half, sub_half), (1, sc_ps, mx_ok, sub_ok)):
                h = by_half[hf]
                dve.wait_ge(ready, 1)
                dve.tensor_reduce(mx[:, 0, h], by_head_ps(0)[:, h, :], AX.X, ALU.max).then_inc(mx_done, 1)
                dve.wait_ge(mx_done, 1)
                dve.tensor_tensor(by_head(first_tile[:, hf, :]), by_head_ps(0)[:, h, :],
                                  mx[:, 0, h].unsqueeze(2).to_broadcast([P, NH // 2, S]), ALU.subtract).then_inc(sub_done, 1)
            split_x(1)
            for hf, ready in ((0, exp_half), (1, exp_ok)):
                dve.wait_ge(ready, 1)
                ins = dve.tensor_reduce(den[:, 0, by_half[hf]], by_head(first_tile[:, hf, :]), AX.X, ALU.add)
            ins.then_inc(den_ok, 1)
            dve.wait_ge(tg_ok, 1)
            dve.wait_ge(prep, 3)
            dve.tensor_scalar(tga[:, :], anyvalid[:, :], tg[:, 0:1], None, ALU.mult)
            reciprocal(0, 0)
            maximum(0, 1)
            dve.tensor_scalar(comb[:, 0:NT], mhalf[:, :], -2.0, tg[:, 1:2], ALU.mult, ALU.mult)
            dve.wait_ge(gwhi_ok, 1)
            dve.tensor_tensor(gw[:, :, NE:], gw_sb[:, :].rearrange("p (k e) -> p k e", k=KD), gw[:, :, 0:NE].bitcast(F32),
                              ALU.subtract).then_inc(gwlo_ok, 1)
            less_max(0, 1)
            maximum(1, 0)
            denominator(0, 1)
            reciprocal(0, 1)
            with dve.Fori(1, NB - 1) as b:
                attend_batch(b)
            b = NB - 1
            split_p(b - 1, 0)
            variance2(0)
            less_max(b, 0)
            denominator(b, 0)
            add_attention(b - 1, 0)
            split_p(b - 1, 1)
            reciprocal(b, 0)
            statistics(b - 1, 0)
            split_x2(1)
            maximum(b, 1)
            split_x2(0)
            less_max(b, 1)
            add_attention(b - 1, 1)
            split_p(b, 0)
            denominator(b, 1)
            statistics(b - 1, 1)
            reciprocal(b, 1)
            variance2(1)
            gate_hidden(0, 0)
            split_hid(0, 0)
            add_attention(b, 0)
            normal_x2(1)
            statistics(b, 0)
            split_p(b, 1)
            variance2(2)
            gate_hidden(1, 1)
            split_x2(2)
            normal_x2(2)
            add_attention(b, 1)
            statistics(b, 1)
            variance2(3)
            split_hid(1, 1)
            normal_x2(3)
            split_x2(3)
            add_expert(0, 0)
            split_w(dve, JS, 0, JS % RS)
            split_w(dve, JS + 1, 1, (JS + 1) % RS)
            dve.wait_ge(lg_ps, 1)
            dve.tensor_reduce(logits[:, :, :], bankS[:, 1, 0:NT * 2 * NE].rearrange("p (t i e) -> p t e i", i=2, e=NE), AX.X,
                              ALU.add).then_inc(route, 1)
            dve.wait_ge(route, 1)
            dve.tensor_reduce(lmax[:, :], logits[:, :, :], AX.X, ALU.max).then_inc(route, 1)
            dve.wait_ge(route, 2)
            dve.tensor_tensor(logits[:, :, :], logits[:, :, :], lmax[:, :].unsqueeze(2).to_broadcast([P, NT, NE]),
                              ALU.subtract).then_inc(route, 1)
            gate_hidden(2, 2)
            gate_hidden(3, 3)
            split_hid(2, 2)

            def weigh_experts():
                dve.wait_ge(lexp_ok, 1)
                dve.tensor_reduce(lsum[:, :], lexp[:, :, :], AX.X, ALU.add).then_inc(route, 1)
                dve.wait_ge(route, 4)
                dve.reciprocal(lrcp[:, :], lsum[:, :]).then_inc(route, 1)
                dve.wait_ge(route, 5)
                dve.tensor_tensor(rp[:, :, :], lexp[:, :, :], lrcp[:, :].unsqueeze(2).to_broadcast([P, NT, NE]),
                                  ALU.mult).then_inc(route, 1)
                dve.wait_ge(route, 6)
                pj = rp[:, :, :].unsqueeze(2).to_broadcast([P, NT, NE, NE])
                pe_ = rp[:, :, :].unsqueeze(3).to_broadcast([P, NT, NE, NE])

                def pairs(ap):
                    return ap[:, :, :].rearrange("p t (e j) -> p t e j", e=NE)

                dve.tensor_tensor(pairs(gt), pj, pe_, ALU.is_gt).then_inc(route, 1)
                dve.tensor_tensor(pairs(eq), pj, pe_, ALU.is_equal).then_inc(route, 1)
                dve.wait_ge(route, 8)
                dve.tensor_tensor(eq[:, :, :], eq[:, :, :], before[:, :].unsqueeze(1).to_broadcast([P, NT, NE * NE]),
                                  ALU.mult).then_inc(route, 1)
                dve.wait_ge(route, 9)
                dve.tensor_tensor(gt[:, :, :], gt[:, :, :], eq[:, :, :], ALU.add).then_inc(route, 1)
                dve.wait_ge(route, 10)
                dve.tensor_reduce(rank[:, :, :], pairs(gt), AX.X, ALU.add).then_inc(route, 1)
                dve.wait_ge(route, 11)
                dve.tensor_scalar(keep[:, :, :], rank[:, :, :], 2.0, tg[:, 1:2], ALU.is_lt, ALU.mult).then_inc(route, 1)
                dve.wait_ge(route, 12)
                dve.tensor_tensor(comb[:, NT:].rearrange("p (e t) -> p t e", t=NT), rp[:, :, :], keep[:, :, :], ALU.mult).then_inc(route, 1)
                dve.wait_ge(route, 13)

            def expert(e, first, last):
                base = e * JE * NC + JS * NC
                for u in range(2 * JE):
                    gate_hidden(base + u, u)
                    split_hid(base + u - 1, u - 1 + 2 * JE)
                    if u < 2 and not (first and u == 0):
                        add_expert(e, u)
                    if first and u == 3:
                        weigh_experts()
                    if u % 2 == 0 and not (last and u >= JE):
                        i = JS + u // 2 + 2
                        split_w(dve, e * JE + i, (i + JS) % WS, i % RS)

            expert(0, True, False)
            with dve.Fori(1, NE - 1) as e:
                expert(e, False, False)
            expert(NE - 1, False, True)
            split_hid(2 * NM - 1, 2 * JE - 1)
            for c in range(NC):
                add_expert(NE, c, True)

        @block.gpsimd
        def _(pool):
            def split_wq(g, s):
                pool.wait_ge(wq_hi, g + 1)
                pool.tensor_tensor(w_lo[:, s, 0:2 * D], raw_kvq[:, s, 2 * HD:KVQ], w_hi[:, s, 0:2 * D].bitcast(F32),
                                   ALU.subtract).then_inc(wq_lo, 1)

            def finish_x(h):
                t0, t1 = HALVES[h]
                pool.wait_ge(vare_ok, h + 1)
                pool.tensor_tensor(rstd[:, t0:t1], vare[:, t0:t1], mhalf[:, t0:t1], ALU.pow).then_inc(rstd_ok, 1)
                pool.wait_ge(rstd_ok, h + 1)
                pool.tensor_tensor(mrneg[:, t0:t1], mneg[:, t0:t1], rstd[:, t0:t1], ALU.mult).then_inc(mrneg_ok, 1)

            for s in range(2):
                split_wq(s, s)
            pool.wait_ge(mhalf_ok, 1)
            for s in range(2):
                split_wq(2 + s, s)
            finish_x(0)
            with pool.Fori(2, NG // 2) as it:
                for s in range(2):
                    split_wq(it * 2 + s, s)
            finish_x(1)
            for t in range(TPB):
                split_w(pool, t, JS + t, t % RS)
                pool.wait_ge(rcp_ok, t + 1)
                normal_p(pool, t)
            with pool.Fori(1, NB - 1) as b:
                for par in range(TPB):
                    pool.wait_ge(rcp_ok, b * TPB + par + 1)
                    normal_p(pool, par)
            for h, (t0, t1) in enumerate(PARTS):
                pool.wait_ge(vare2_ok, h + 1)
                pool.tensor_tensor(rstd2[:, t0:t1], vare2[:, t0:t1], mhalf[:, t0:t1], ALU.pow).then_inc(rstd2_ok, 1)
                if h == 0:
                    pool.wait_ge(rstd2_ok, 1)
                    pool.tensor_tensor(mrneg2[:, t0:t1], mneg2[:, t0:t1], rstd2[:, t0:t1], ALU.mult).then_inc(mrneg2_ok, 1)
                    for par in range(TPB):
                        pool.wait_ge(rcp_ok, NT - TPB + par + 1)
                        normal_p(pool, par)
            pool.wait_ge(route, 3)
            pool.tensor_tensor(lexp[:, :, :], euler[:, :].rearrange("p (t e) -> p t e", e=NE), logits[:, :, :],
                               ALU.pow).then_inc(lexp_ok, 1)


def kernel(x, ctx_1024, mask_BxS2_bf1, g_xattn, g_ffn, L0_xattn_Wq, L0_xattn_Wk, L0_xattn_Wv, L0_xattn_Wo,
           L0_ffn_gate_w, L0_ffn_w1, L0_ffn_w3, L0_ffn_w2, L0_ffn_sw1, L0_ffn_sw3, L0_ffn_sw2):
    import numpy as np
    import concourse.bacc as bacc
    from concourse import mybir as _mybir
    from concourse.bass_utils import run_bass_kernel_spmd

    a = np.asarray
    kv = [a(w).reshape(DV, NG, HD).transpose(1, 0, 2) for w in (L0_xattn_Wk, L0_xattn_Wv)]
    ctxT = a(ctx_1024).transpose(2, 0, 1).reshape(DV, NB * S)
    wqT = a(L0_xattn_Wq).reshape(D, NG, 2, HD).transpose(1, 3, 2, 0).reshape(NG, HD, 2 * D)
    wo = a(L0_xattn_Wo).reshape(NG, 2, HD, D).transpose(0, 2, 1, 3).reshape(NG, HD, 2 * D)

    def hidden_tiles(w1, w3, w2):
        n = w1.shape[0] // P
        ups = [w.reshape(n, P, KD, P).transpose(0, 3, 2, 1).reshape(n, P, KD * P) for w in (w1, w3)]
        return np.concatenate(ups + [w2.T.reshape(n, P, D)], axis=2)

    tiles = [hidden_tiles(a(L0_ffn_sw1), a(L0_ffn_sw3), a(L0_ffn_sw2))]
    tiles += [hidden_tiles(a(L0_ffn_w1)[e], a(L0_ffn_w3)[e], a(L0_ffn_w2)[e]) for e in range(NE)]
    e, j = np.meshgrid(np.arange(NE), np.arange(NE), indexing="ij")
    arrays = {
        "x": a(x).reshape(NB * T, D),
        "ctxT_kv0": np.concatenate([ctxT, kv[0][0], kv[1][0]], axis=1),
        "mask": np.broadcast_to(a(mask_BxS2_bf1).view(np.uint8).reshape(1, NB * S), (P, NB * S)),
        "gates": np.broadcast_to(np.concatenate([a(g_xattn), a(g_ffn)]).reshape(1, 2), (P, 2)),
        "kvq": np.concatenate(kv + [wqT], axis=2),
        "wo": wo,
        "gwT": a(L0_ffn_gate_w).reshape(NE, KD, P).transpose(2, 1, 0).reshape(P, KD * NE),
        "ffn": np.concatenate(tiles, axis=0),
        "ident": np.eye(P, dtype=np.float32),
        "before": np.broadcast_to((j < e).astype(np.float32).reshape(1, NE * NE), (P, NE * NE)),
    }
    nc = bacc.Bacc("TRN2", target_bir_lowering=False, num_devices=1)
    feed, args = {}, []
    for name, v in arrays.items():
        v = np.ascontiguousarray(v)
        feed[f"{name}_dram"] = v
        args.append(nc.dram_tensor(f"{name}_dram", v.shape, _mybir.dt.from_np(v.dtype), kind="ExternalInput").ap())
    out = nc.dram_tensor("out_dram", (NB * T, D), F32, kind="ExternalOutput").ap()
    build(nc, *args, out)
    r = run_bass_kernel_spmd(nc, [feed], core_ids=[0])
    return r.results[0]["out_dram"].reshape(NB, T, D)
```
